# Optimizing a Trainium2 kernel written in Bass

```python
import numpy as np
import jax
import jax.numpy as jnp

def _softmax(x, axis=-1):
    return jax.nn.softmax(x, axis=axis)

def _gelu(x):
    return jax.nn.gelu(x, approximate=True)

def _silu(x):
    return jax.nn.silu(x)

def _sigmoid(x):
    return jax.nn.sigmoid(x)

def _layernorm(x, axis=-1, eps=1e-05):
    m = jnp.mean(x, axis=axis, keepdims=True)
    v = jnp.var(x, axis=axis, keepdims=True)
    return (x - m) / jnp.sqrt(v + eps)

def _scatter_add(tgt, idx, src, axis=0):
    return tgt.at[idx].add(src)

def _segment_sum(src, seg, n):
    return jax.ops.segment_sum(src, seg, n)
kernel_name = 'mk_adj_seq_d1_adj_r2_d04b78'

def setup_inputs(seed: int=0):
    np.random.seed(seed)
    _w = jnp.asarray

    def _rec_inputs():
        import jax
        import jax.numpy as jnp
        _gk = jax.random.key(seed)
        x = -0.0005207 + 1.001 * jax.random.normal(jax.random.fold_in(_gk, 1), (2048, 256), jnp.float32)
        _a = jax.random.bernoulli(jax.random.fold_in(_gk, 2), 0.00195312, (2048, 2048))
        adj = _a.astype(jnp.int32)
        return (x, adj)
    x, adj = _rec_inputs()

    def _L0_gnn_setup():
        import jax, jax.numpy as jnp
        import numpy as np
        D_MODEL = 256
        N_HEADS = 8
        D_K = D_MODEL // N_HEADS
        D_FF = 1024
        N = 2048
        EPS = 1e-05

        def _layer_norm(x, g, b):
            mu = jnp.mean(x, axis=-1, keepdims=True)
            var = jnp.mean(jnp.square(x - mu), axis=-1, keepdims=True)
            return (x - mu) * jax.lax.rsqrt(var + EPS) * g + b
        key = jax.random.key(seed)
        ks = jax.random.split(key, 16)
        s = 1.0 / np.sqrt(D_MODEL)
        sf = 1.0 / np.sqrt(D_FF)
        inp = {'h': jax.random.normal(ks[0], (N, D_MODEL), dtype=jnp.float32), 'adj': jax.random.randint(ks[1], (N, N), 0, 2, dtype=jnp.int32), 'Wq': jax.random.uniform(ks[2], (D_MODEL, D_MODEL), jnp.float32, -s, s), 'bq': jnp.zeros((D_MODEL,), jnp.float32), 'Wk': jax.random.uniform(ks[3], (D_MODEL, D_MODEL), jnp.float32, -s, s), 'bk': jnp.zeros((D_MODEL,), jnp.float32), 'Wv': jax.random.uniform(ks[4], (D_MODEL, D_MODEL), jnp.float32, -s, s), 'bv': jnp.zeros((D_MODEL,), jnp.float32), 'Wo': jax.random.uniform(ks[5], (D_MODEL, D_MODEL), jnp.float32, -s, s), 'bo': jnp.zeros((D_MODEL,), jnp.float32), 'W1': jax.random.uniform(ks[6], (D_FF, D_MODEL), jnp.float32, -s, s), 'b1': jnp.zeros((D_FF,), jnp.float32), 'W2': jax.random.uniform(ks[7], (D_MODEL, D_FF), jnp.float32, -sf, sf), 'b2': jnp.zeros((D_MODEL,), jnp.float32), 'ln1_g': jnp.ones((D_MODEL,), jnp.float32), 'ln1_b': jnp.zeros((D_MODEL,), jnp.float32), 'ln2_g': jnp.ones((D_MODEL,), jnp.float32), 'ln2_b': jnp.zeros((D_MODEL,), jnp.float32)}
        return inp
    _L0_gnn_all = _L0_gnn_setup()
    _L0_gnn_in = {k: v for k, v in _L0_gnn_all.items() if k in ('Wq', 'bq', 'Wk', 'bk', 'Wv', 'bv', 'Wo', 'bo', 'W1', 'b1', 'W2', 'b2', 'ln1_g', 'ln1_b', 'ln2_g', 'ln2_b')}
    del _L0_gnn_all
    return {'x': x, 'adj': adj, 'L0_gnn_Wq': _L0_gnn_in['Wq'], 'L0_gnn_bq': _L0_gnn_in['bq'], 'L0_gnn_Wk': _L0_gnn_in['Wk'], 'L0_gnn_bk': _L0_gnn_in['bk'], 'L0_gnn_Wv': _L0_gnn_in['Wv'], 'L0_gnn_bv': _L0_gnn_in['bv'], 'L0_gnn_Wo': _L0_gnn_in['Wo'], 'L0_gnn_bo': _L0_gnn_in['bo'], 'L0_gnn_W1': _L0_gnn_in['W1'], 'L0_gnn_b1': _L0_gnn_in['b1'], 'L0_gnn_W2': _L0_gnn_in['W2'], 'L0_gnn_b2': _L0_gnn_in['b2'], 'L0_gnn_ln1_g': _L0_gnn_in['ln1_g'], 'L0_gnn_ln1_b': _L0_gnn_in['ln1_b'], 'L0_gnn_ln2_g': _L0_gnn_in['ln2_g'], 'L0_gnn_ln2_b': _L0_gnn_in['ln2_b']}

def reference(x, adj, L0_gnn_Wq, L0_gnn_bq, L0_gnn_Wk, L0_gnn_bk, L0_gnn_Wv, L0_gnn_bv, L0_gnn_Wo, L0_gnn_bo, L0_gnn_W1, L0_gnn_b1, L0_gnn_W2, L0_gnn_b2, L0_gnn_ln1_g, L0_gnn_ln1_b, L0_gnn_ln2_g, L0_gnn_ln2_b):
    import jax
    import jax.numpy as jnp

    def _L0_gnn_ref(h, adj, Wq, bq, Wk, bk, Wv, bv, Wo, bo, W1, b1, W2, b2, ln1_g, ln1_b, ln2_g, ln2_b):
        import jax, jax.numpy as jnp
        import numpy as np
        D_MODEL = 256
        N_HEADS = 8
        D_K = D_MODEL // N_HEADS
        D_FF = 1024
        N = 2048
        EPS = 1e-05

        def _layer_norm(x, g, b):
            mu = jnp.mean(x, axis=-1, keepdims=True)
            var = jnp.mean(jnp.square(x - mu), axis=-1, keepdims=True)
            return (x - mu) * jax.lax.rsqrt(var + EPS) * g + b
        n = h.shape[0]
        mask = adj.astype(jnp.float32) + jnp.eye(n, dtype=jnp.float32)
        q = (h @ Wq.T + bq).reshape(n, N_HEADS, D_K)
        k = (h @ Wk.T + bk).reshape(n, N_HEADS, D_K)
        v = (h @ Wv.T + bv).reshape(n, N_HEADS, D_K)
        scores = jnp.einsum('nhd,mhd->hnm', q, k) / jnp.sqrt(jnp.float32(D_K))
        scores = jnp.where(mask[None, :, :] == 0, jnp.float32(-1000000000.0), scores)
        attn = jax.nn.softmax(scores, axis=-1)
        ctx = jnp.einsum('hnm,mhd->nhd', attn, v).reshape(n, D_MODEL)
        attn_out = ctx @ Wo.T + bo
        h1 = _layer_norm(h + attn_out, ln1_g, ln1_b)
        ff = jax.nn.relu(h1 @ W1.T + b1) @ W2.T + b2
        h2 = _layer_norm(h1 + ff, ln2_g, ln2_b)
        return h2
    x = _L0_gnn_ref(x, adj, L0_gnn_Wq, L0_gnn_bq, L0_gnn_Wk, L0_gnn_bk, L0_gnn_Wv, L0_gnn_bv, L0_gnn_Wo, L0_gnn_bo, L0_gnn_W1, L0_gnn_b1, L0_gnn_W2, L0_gnn_b2, L0_gnn_ln1_g, L0_gnn_ln1_b, L0_gnn_ln2_g, L0_gnn_ln2_b)
    return x

_drawn_inputs = setup_inputs


def setup_inputs(seed=0):
    import zlib

    import numpy as np

    out = dict(_drawn_inputs(seed))
    spreads = {'L0_gnn_bq': (0.0, 0.8),
     'L0_gnn_bk': (0.0, 0.8),
     'L0_gnn_bv': (0.0, 0.1),
     'L0_gnn_bo': (0.0, 0.1),
     'L0_gnn_b1': (0.0, 0.1),
     'L0_gnn_b2': (0.0, 0.1),
     'L0_gnn_ln1_g': (1.0, 0.2),
     'L0_gnn_ln1_b': (0.0, 0.1),
     'L0_gnn_ln2_g': (1.0, 0.2),
     'L0_gnn_ln2_b': (0.0, 0.1)}
    factors = {}
    for name, (base, spread) in spreads.items():
        noise = np.random.default_rng([zlib.crc32(name.encode()), seed]).standard_normal(out[name].shape)
        drawn = base * np.exp(spread * noise) if base else spread * noise
        out[name] = jnp.asarray(drawn.astype(out[name].dtype))
    for name, factor in factors.items():
        out[name] = (out[name] * factor).astype(out[name].dtype)
    return out
```

```python
from contextlib import ExitStack

import concourse.bass as bass
from concourse import mybir

F32 = mybir.dt.float32
F16 = mybir.dt.float16
BF16 = mybir.dt.bfloat16
I32 = mybir.dt.int32
ALU = mybir.AluOpType
ACT = mybir.ActivationFunctionType
AX = mybir.AxisListType

P = 128
N = 2048
D = 256
H = 8
DK = D // H
FF = 1024
T = N // P
KD = D // P
FB = FF // P
SLOTS = 8
LIST = 16
QUARTER = N // 4
SELF = SLOTS
VIRT = SLOTS + 1
ALLS = SLOTS + 2
SCALE = 1.0 / float(DK) ** 0.5
EPS = 1e-5
FAR = 4096
MASKED = -1e30
VCOLS = D + 2 * H + 1
BIAS = 5 * D
ADJ_RING = 4
LAG = 5


def build(nc, x, x_t, adj, w_kvq, bias_row, w_o, w_1, b_1, w_2, ln_rows, out):
    kv_table = nc.dram_tensor("kv_table", (N, 2 * D), F32).ap()
    with ExitStack() as ctx:
        def sb(name, shape, dt=F32):
            return ctx.enter_context(nc.sbuf_tensor(name, shape, dt))

        def sem(name):
            return ctx.enter_context(nc.semaphore(name))

        wkvq = sb("wkvq", [P, KD, 3 * D])
        wo = sb("wo", [P, KD, D])
        w1 = sb("w1", [P, KD, FF])
        w2 = sb("w2", [P, FB, D])
        b1 = sb("b1", [P, FB])
        ln = sb("ln", [P, 4, D])
        bias_parts = sb("bias_parts", [96, BIAS], BF16)
        ones_bf = sb("ones_bf", [P, P], BF16)
        ones = sb("ones", [P, P])
        eye = sb("eye", [P, P])
        not_eye_i = sb("not_eye_i", [P, P], I32)
        not_eye = sb("not_eye", [P, P])
        before = sb("before", [P, P])
        col_no = sb("col_no", [P, N], F16)
        minus_half = sb("minus_half", [P, 1])
        kv = sb("kv", [P, T, 2 * D])
        q = sb("q", [P, T, D])
        lists = sb("lists", [P, T, LIST + 1])
        idx = sb("idx", [P, T, LIST])
        mask = sb("mask", [P, T, LIST])
        count = sb("count", [P, T])
        xt = sb("xt", [P, ADJ_RING, KD, P])
        adj_ring = sb("adj_ring", [P, ADJ_RING, N], I32)
        coded = sb("coded", [P, 2, N], F16)
        cand = sb("cand", [P, 2, 32])
        cand_rest = sb("cand_rest", [P, 2, 32])
        top = sb("top", [P, 2, LIST])
        gath = sb("gath", [P, 2, SLOTS, 2 * D])
        idx_ring = sb("idx_ring", [P, 2, SLOTS], I32)
        prod = sb("prod", [P, SLOTS + 1, D])
        pv = sb("pv", [P, 2, ALLS, D])
        sc = sb("sc", [P, ALLS, H])
        ex = sb("ex", [P, ALLS, H])
        wts = sb("wts", [P, ALLS, H])
        mx = sb("mx", [P, H])
        lsum = sb("lsum", [P, H])
        rinv = sb("rinv", [P, H])
        absent = sb("absent", [P, 1])
        turned = sb("turned", [P, 2, P])
        vdata = sb("vdata", [P, VCOLS])
        vlist = sb("vlist", [P, SLOTS + 1])
        vq = sb("vq", [P, D])
        vidx = sb("vidx", [P, SLOTS], I32)
        vmask = sb("vmask", [P, SLOTS])
        small = sb("small", [P, 8, T])
        flag_i = sb("flag_i", [1, 1], I32)
        ctx_t = sb("ctx_t", [P, KD, P])
        xr = sb("xr", [P, 2, D])
        lntmp = sb("lntmp", [P, D])
        h1 = sb("h1", [P, 2, D])
        h1_t = sb("h1_t", [P, KD, 2, P])
        stats = sb("stats", [P, 2, 6])
        mv1 = sb("mv1", [P, 2, 2])
        mv2 = sb("mv2", [P, 2, 2])
        rstd1 = sb("rstd1", [P, 2, 2])
        rstd2 = sb("rstd2", [P, 2, 2])
        onehot = adj_ring[:, 0].bitcast(F32).rearrange("p (t n) -> p t n", t=T)
        hid = coded[:].rearrange("p a n -> p (a n)").bitcast(F32).rearrange("p (f a n) -> p f a n", f=FB, a=2)
        h1keep = xt[:].rearrange("p r k n -> p r (k n)")
        spent = wkvq[:].rearrange("p k n -> p (k n)").rearrange("p (a u d) -> p a u d", a=3, u=2)
        r1, r2, outs = spent[:, 0], spent[:, 1], spent[:, 2]
        raw = gath[:, 0].rearrange("p s d -> p (s d)")
        b_raw = raw[0:96, 0:BIAS]
        b_rest = raw[0:96, BIAS:2 * BIAS]
        b_hi = raw[0:96, 2 * BIAS:2 * BIAS + BIAS // 2].bitcast(BF16)
        b_mid = raw[0:96, 2 * BIAS + BIAS // 2:3 * BIAS].bitcast(BF16)
        d_mask = adj_ring[:, 1].bitcast(F32)
        d_sc = adj_ring[:, 2].bitcast(F32)
        d_p = adj_ring[:, 3].bitcast(F32)
        d_k = prod[:, 0:2, :].rearrange("p a (b d) -> p (a b) d", d=DK)
        d_q = prod[:, 2, 0:DK]
        d_qt = prod[0:DK, 3, 0:P]
        d_t = prod[:, 4:6, :].rearrange("p a b -> p (a b)")

        psum = ctx.enter_context(nc.psum_tensor("psum", [P, 8, 512], F32))
        bank = [psum[:, b] for b in range(8)]

        weights_in = sem("weights_in")
        biases_in = sem("biases_in")
        late_weights_in = sem("late_weights_in")
        xt_in = [sem(f"xt_in{i}") for i in range(ADJ_RING)]
        adj_in = [sem(f"adj_in{i}") for i in range(ADJ_RING)]
        xr_in = [sem(f"xr_in{i}") for i in range(2)]
        gathered = [sem(f"gathered{i}") for i in range(2)]
        v_gathered = sem("v_gathered")
        dense_adj_in = sem("dense_adj_in")
        bias_zeroed = sem("bias_zeroed")
        pool_consts = sem("pool_consts")
        bias_step = sem("bias_step")
        kv_product = sem("kv_product")
        q_product = sem("q_product")
        kv_stored = sem("kv_stored")
        q_stored = sem("q_stored")
        table_written = sem("table_written")
        diag_cleared = sem("diag_cleared")
        mask_cast = sem("mask_cast")
        coded_ready = sem("coded_ready")
        cands_ready = sem("cands_ready")
        tops_ready = sem("tops_ready")
        rest_ready = sem("rest_ready")
        listed = sem("listed")
        lists_done = sem("lists_done")
        prep = sem("prep")
        prep_pe = sem("prep_pe")
        onehots = sem("onehots")
        flag_ready = sem("flag_ready")
        idx_ready = sem("idx_ready")
        idx_staged = sem("idx_staged")
        vrows_ready = sem("vrows_ready")
        vidx_ready = sem("vidx_ready")
        v_step = sem("v_step")
        v_shifted = sem("v_shifted")
        v_exp = sem("v_exp")
        v_done = sem("v_done")
        turned_ready = sem("turned_ready")
        merged = sem("merged")
        prods_ready = sem("prods_ready")
        sm_step = sem("sm_step")
        shifted = sem("shifted")
        exp_done = sem("exp_done")
        sm_step2 = sem("sm_step2")
        pv_ready = sem("pv_ready")
        ctx_summed = sem("ctx_summed")
        ctx_copied = sem("ctx_copied")
        wo_done = sem("wo_done")
        r1_ready = sem("r1_ready")
        stats1 = sem("stats1")
        mv1_ready = sem("mv1_ready")
        var1_ready = sem("var1_ready")
        rstd1_ready = sem("rstd1_ready")
        half1 = sem("half1")
        h1_ready = sem("h1_ready")
        h1_turned = sem("h1_turned")
        h1_copied = sem("h1_copied")
        ff1_ready = sem("ff1_ready")
        relu_done = sem("relu_done")
        ff2_done = sem("ff2_done")
        r2_ready = sem("r2_ready")
        stats2 = sem("stats2")
        mv2_ready = sem("mv2_ready")
        var2_ready = sem("var2_ready")
        rstd2_ready = sem("rstd2_ready")
        half2 = sem("half2")
        out_ready = sem("out_ready")
        stored = [sem(f"stored{i}") for i in range(2)]
        d_mask_step = sem("d_mask_step")
        d_staged = sem("d_staged")
        d_product = sem("d_product")
        d_max = sem("d_max")
        d_exp = sem("d_exp")
        d_inv = sem("d_inv")
        d_done = sem("d_done")
        passed = sem("passed")

        block = ctx.enter_context(nc.Block())

        def wait(eng, s, value):
            if not isinstance(value, int) or value > 0:
                eng.wait_ge(s, value)

        def wait_alone(eng, s, value):
            eng.wait_ge(s, value)
            eng.sem_inc(passed, 1)

        def steps(eng, step):
            for t in range(0, LAG + 1):
                step(t, t % 2)
            with eng.Fori((LAG + 1) // 2, T // 2) as g:
                t = g * 2
                step(t, 0)
                step(t + 1, 1)
            for t in range(T, T + LAG):
                step(t, t % 2)

        def on(t, lag):
            return not isinstance(t, int) or 0 <= t - lag < T

        def both_ways(eng, fast, dense):
            eng.wait_ge(flag_ready, 1)
            flag = eng.value_load(flag_i[0:1, 0:1], min_val=0, max_val=1)
            with eng.If(flag < 1):
                fast()
            with eng.Else():
                dense()

        @block.sync
        def _(sp):
            sp.dma_start(wkvq[:], w_kvq.rearrange("(k p) n -> p k n", p=P)).then_inc(weights_in, 16)
            for r in range(ADJ_RING):
                sp.dma_start(xt[:, r], x_t[r].rearrange("p (k n) -> p k n", k=KD)).then_inc(xt_in[r], 16)
            for r in range(ADJ_RING):
                sp.dma_start(adj_ring[:, r], adj[bass.ts(r, P), :]).then_inc(adj_in[r], 16)
            with sp.Fori(1, T // ADJ_RING) as g:
                i = g * ADJ_RING
                for r in range(ADJ_RING):
                    sp.wait_ge(q_product, i + (r + 1 - ADJ_RING))
                    sp.dma_start(xt[:, r], x_t[bass.ds(i + r, 1)].rearrange("t p (k n) -> p (t k) n", k=KD)).then_inc(xt_in[r], 16)
                    sp.wait_ge(mask_cast, i + (r + 1 - ADJ_RING))
                    sp.dma_start(adj_ring[:, r], adj[bass.ds((i + r) * P, P), :]).then_inc(adj_in[r], 16)
            sp.dma_start(wo[:], w_o.rearrange("(k p) n -> p k n", p=P)).then_inc(late_weights_in, 16)
            sp.dma_start(w1[:], w_1.rearrange("(k p) n -> p k n", p=P)).then_inc(late_weights_in, 16)
            sp.dma_start(w2[:], w_2.rearrange("(k p) n -> p k n", p=P)).then_inc(late_weights_in, 16)
            sp.dma_start(b1[:], b_1).then_inc(late_weights_in, 16)
            for r in range(4):
                sp.dma_start(ln[:, r], ln_rows[r:r + 1, :].to_broadcast([P, D])).then_inc(late_weights_in, 16)

            def step(t, u, dense):
                if on(t, 0):
                    wait(sp, r1_ready, t - 1)
                    sp.dma_start(xr[:, u], x[bass.ds(t * P, P), :]).then_inc(xr_in[u], 16)
                    if dense:
                        wait(sp, d_mask_step, 2 * t)
                        sp.dma_start(adj_ring[:, 0], adj[bass.ds(t * P, P), :]).then_inc(dense_adj_in, 16)
                if on(t, LAG):
                    sp.wait_ge(out_ready, t - (LAG - 1))
                    sp.dma_start(out[bass.ds((t - LAG) * P, P), :], outs[:, 1 - u]).then_inc(stored[1 - u], 16)

            both_ways(sp, lambda: steps(sp, lambda t, u: step(t, u, False)),
                      lambda: steps(sp, lambda t, u: step(t, u, True)))
            for u in range(2):
                sp.wait_ge(stored[u], 16 * T // 2)

        @block.gpsimd
        def _(pool):
            nc.gpsimd.memset(b_raw, 0.0).then_inc(bias_zeroed, 1)
            nc.gpsimd.memset(not_eye_i[:], 1).then_inc(pool_consts, 1)
            nc.gpsimd.iota(col_no[:], [[1, N]], base=1, channel_multiplier=0,
                           allow_small_or_imprecise_dtypes=True).then_inc(pool_consts, 1)
            nc.gpsimd.memset(ones[:], 1.0).then_inc(pool_consts, 1)
            nc.gpsimd.memset(ones_bf[:], 1.0).then_inc(pool_consts, 1)
            nc.gpsimd.memset(eye[:], 0.0).then_inc(pool_consts, 1)
            nc.gpsimd.iota(lists[:, :, LIST], [[P, T]], base=1, channel_multiplier=1,
                           allow_small_or_imprecise_dtypes=True).then_inc(pool_consts, 1)
            nc.gpsimd.memset(minus_half[:], -0.5).then_inc(pool_consts, 1)
            pool.wait_ge(pool_consts, 7)
            nc.gpsimd.affine_select(out=not_eye_i[:], in_=not_eye_i[:], compare_op=ALU.not_equal, fill=0.0,
                                    base=0, pattern=[[-1, P]], channel_multiplier=1).then_inc(pool_consts, 1)
            nc.gpsimd.affine_select(out=not_eye[:], in_=ones[:], compare_op=ALU.not_equal, fill=0.0,
                                    base=0, pattern=[[-1, P]], channel_multiplier=1).then_inc(pool_consts, 1)
            nc.gpsimd.affine_select(out=eye[:], in_=eye[:], compare_op=ALU.not_equal, fill=1.0,
                                    base=0, pattern=[[-1, P]], channel_multiplier=1).then_inc(pool_consts, 1)
            nc.gpsimd.affine_select(out=before[:], in_=ones[:], compare_op=ALU.is_gt, fill=0.0,
                                    base=0, pattern=[[1, P]], channel_multiplier=-1).then_inc(pool_consts, 1)
            pool.wait_ge(pool_consts, 11)
            with pool.Fori(0, T // ADJ_RING) as g:
                i = g * ADJ_RING
                for r in range(ADJ_RING):
                    pool.wait_ge(adj_in[r], i * (16 // ADJ_RING) + 16)
                    blk = adj_ring[:, r, bass.ds((i + r) * P, P)]
                    nc.gpsimd.tensor_tensor(blk, blk, not_eye_i[:], ALU.mult).then_inc(diag_cleared, 1)
            pool.wait_ge(bias_step, 6)
            nc.gpsimd.memset(gath[:, 1], 0.0).then_inc(prep, 1)
            nc.gpsimd.memset(raw[:, :], 0.0).then_inc(prep, 1)
            pool.wait_ge(table_written, 16 * T)

            def rows_of(ix, dst, done):
                for s in range(SLOTS):
                    pool.indirect_dma_start(dst[:, s, :], None, kv_table,
                                            bass.IndirectOffsetOnAxis(ap=ix[:, s:s + 1], axis=0),
                                            bounds_check=N - 1, oob_is_err=False).then_inc(done, 16)

            def gather(t, u):
                wait_alone(pool, idx_staged, t + 1)
                if not isinstance(t, int) or t > 1:
                    wait_alone(pool, pv_ready, t - 1)
                rows_of(idx_ring[:, u], gath[:, u], gathered[u])

            def rstd(t, u, mv, res, mv_sem, var_sem, res_sem):
                wait_alone(pool, mv_sem, t + 1)
                nc.gpsimd.tensor_scalar(res[:, u, 0:1], mv[:, u, 1:2], EPS, None, ALU.add).then_inc(var_sem, 1)
                pool.wait_ge(var_sem, t + 1)
                nc.gpsimd.tensor_tensor(res[:, u, 1:2], res[:, u, 0:1], minus_half[:], ALU.pow).then_inc(res_sem, 1)

            def step(t, u, dense):
                if on(t + 1, 0) and on(t, 0) and not dense and not (isinstance(t, int) and t == 0):
                    if isinstance(t, int):
                        gather(t + 1, 1 - u)
                    else:
                        gather(t + 1, 1 - u)
                if on(t, 1):
                    rstd(t - 1, 1 - u, mv1, rstd1, mv1_ready, var1_ready, rstd1_ready)
                if on(t, LAG):
                    rstd(t - LAG, 1 - u, mv2, rstd2, mv2_ready, var2_ready, rstd2_ready)

            def fast():
                pool.wait_ge(prep, 2)
                gather(0, 0)
                pool.wait_ge(vidx_ready, 1)
                rows_of(vidx[:], gath[:, 1], v_gathered)
                pool.wait_ge(v_done, 1)
                gather(1, 1)
                steps_ahead(pool, step)

            def steps_ahead(eng, step):
                for t in range(0, LAG + 1):
                    step(t, t % 2, False)
                with eng.Fori((LAG + 1) // 2, (T - 2) // 2) as g:
                    t = g * 2
                    step(t, 0, False)
                    step(t + 1, 1, False)
                for t in range(T - 2, T + LAG):
                    step(t, t % 2, False)

            both_ways(pool, fast, lambda: steps(pool, lambda t, u: step(t, u, True)))

        @block.tensor
        def _(pe):
            mm, tr = nc.tensor.matmul, nc.tensor.transpose

            def bias(dst, first, at):
                mm(dst, ones_bf[0:96, :], bias_parts[:, at:at + dst.shape[-1]], start=first, stop=False)

            pe.wait_ge(weights_in, 16)
            pe.wait_ge(pool_consts, 11)
            pe.wait_ge(bias_step, 8)
            with pe.Fori(0, T // ADJ_RING) as g:
                i = g * ADJ_RING
                for r in range(ADJ_RING):
                    b = r % 2
                    pe.wait_ge(xt_in[r], i * (16 // ADJ_RING) + 16)
                    pe.wait_ge(kv_stored, i + (r + 1))
                    bias(bank[b], True, 0)
                    for k in range(KD):
                        last = mm(bank[b], xt[:, r, k], wkvq[:, k, 0:2 * D], start=False, stop=k == KD - 1)
                    last.then_inc(kv_product, 1)
                    pe.wait_ge(q_stored, i + (r + 1))
                    bias(bank[2 + b][:, 0:D], True, 2 * D)
                    for k in range(KD):
                        last = mm(bank[2 + b][:, 0:D], xt[:, r, k], wkvq[:, k, 2 * D:3 * D], start=False, stop=k == KD - 1)
                    last.then_inc(q_product, 1)

            pe.wait_ge(prep, 5)
            mm(bank[7][0:T, 0:P], small[:, 0], ones[:], start=True, stop=True).then_inc(prep_pe, 1)
            pe.wait_ge(prep, 6)
            mm(bank[6][:, 0:T], before[:], small[:, 0], start=True, stop=False)
            mm(bank[6][:, 0:T], vdata[0:T, 0:P], before[0:T, 0:T], start=False, stop=True).then_inc(prep_pe, 1)
            mm(bank[5][0:1, 0:2], ones[:, 0:1], small[:, 4, 0:2], start=True, stop=True).then_inc(prep_pe, 1)

            def post(t, u, first=None):
                if on(t, 1):
                    pe.wait_ge(pv_ready, t)
                    if first and on(t, 0):
                        first(t, u)
                    wait(pe, ctx_copied, t - 1)
                    for k in range(KD):
                        for s in range(ALLS):
                            last = mm(bank[1][:, bass.ts(k, P)], pv[:, 1 - u, s, bass.ts(k, P)], eye[:],
                                      start=k == 0 and s == 0, stop=s == ALLS - 1, skip_group_check=True)
                    last.then_inc(ctx_summed, 1)
                if on(t, 1):
                    pe.wait_ge(ctx_copied, t)
                    wait(pe, r1_ready, t - 1)
                    bias(bank[2][:, 0:D], True, 3 * D)
                    for k in range(KD):
                        last = mm(bank[2][:, 0:D], ctx_t[:, k], wo[:, k], start=False, stop=k == KD - 1)
                    last.then_inc(wo_done, 1)
                if u == 1 and on(t, 3):
                    pe.wait_ge(h1_copied, t - 1)
                    for g in range(FB // 2):
                        wait(pe, relu_done, 2 * (t - 3) + g - 1)
                        for j in range(2):
                            for k in range(KD):
                                f = 2 * g + j
                                last = mm(bank[4 + g % 2][:, bass.ts(j, 2 * P)], w1[:, k, bass.ts(f, P)],
                                          h1_t[:, k].rearrange("p a b -> p (a b)"),
                                          start=k == 0 and j == 0, stop=k == KD - 1, skip_group_check=True)
                        last.then_inc(ff1_ready, 1)
                if u == 0 and on(t, 4):
                    pe.wait_ge(relu_done, 2 * (t - 4) + FB // 2)
                    for v in range(2):
                        wait(pe, r2_ready, t - 5 + v)
                        bias(bank[6 + v][:, 0:D], True, 4 * D)
                        for f in range(FB):
                            last = mm(bank[6 + v][:, 0:D], hid[:, f, v], w2[:, f], start=False, stop=f == FB - 1)
                        last.then_inc(ff2_done, 1)
                if on(t, 1):
                    pe.wait_ge(h1_ready, t)
                    wait(pe, h1_copied, t - 1)
                    for k in range(KD):
                        last = tr(bank[3][:, bass.ts(k, P)], h1[:, 1 - u, bass.ts(k, P)], eye[:])
                    last.then_inc(h1_turned, 1)


            def fetch_virtual(t, u):
                pe.wait_ge(turned_ready, t + 1)
                wait(pe, pv_ready, t)
                mm(bank[0][:, 0:VCOLS], turned[:, u], vdata[:], start=True, stop=True).then_inc(merged, 1)

            def fast():
                pe.wait_ge(onehots, T)
                pe.wait_ge(q_stored, T + 2)
                for t in range(T):
                    mm(bank[4][:, 0:D], onehot[:, t], q[:, t], start=t == 0, stop=t == T - 1)
                for t in range(T):
                    last = mm(bank[5][:, 0:SLOTS + 1], onehot[:, t], lists[:, t, SLOTS:LIST + 1],
                              start=t == 0, stop=t == T - 1)
                last.then_inc(vrows_ready, 1)
                pe.wait_ge(v_done, 1)
                fetch_virtual(0, 0)

                steps(pe, lambda t, u: post(t, u, fetch_virtual))

            def dense():
                def heads(t):
                    if not isinstance(t, int) or t > 1:
                        wait_alone(pe, ctx_copied, t - 1)
                    with pe.Fori(0, H) as h:
                        n = t * H + h
                        k0, m0 = n * 10, n * 14
                        pe.wait_ge(d_staged, k0 + 1)
                        tr(bank[1][0:DK, 0:P], d_q, eye[:]).then_inc(d_product, 1)
                        for c in range(4):
                            pe.wait_ge(d_staged, k0 + 2 + c)
                            for j in range(4):
                                last = tr(bank[1][0:DK, bass.ts(j, P)], d_k[:, 4 * c + j], eye[:])
                            last.then_inc(d_product, 1)
                            pe.wait_ge(d_staged, k0 + 3 + c)
                            mm(bank[0], d_qt, d_t[0:DK], start=True, stop=True).then_inc(d_product, 1)
                        pe.wait_ge(d_exp, n + 1)
                        for c in range(4):
                            if c:
                                pe.wait_ge(d_staged, k0 + 6 + c)
                            for j in range(4):
                                last = tr(bank[1][:, bass.ts(j, P)], d_p[:, bass.ts(4 * c + j, P)], eye[:])
                            last.then_inc(d_product, 1)
                            pe.wait_ge(d_staged, k0 + 7 + c)
                            for j in range(4):
                                m = 4 * c + j
                                last = mm(bank[0][:, 0:DK], d_t[:, bass.ts(j, P)],
                                          kv[:, m, bass.ds(h * DK + D, DK)], start=m == 0, stop=m == T - 1)
                        last.then_inc(d_product, 1)

                def step(t, u):
                    if on(t, 0):
                        heads(t)
                    post(t, u)
                steps(pe, step)

            pe.wait_ge(late_weights_in, 16 * 8)
            both_ways(pe, fast, dense)

        @block.scalar
        def _(act):
            af = nc.scalar.activation
            act.wait_ge(bias_zeroed, 1)
            for r in range(3):
                act.dma_start(b_raw[32 * r:32 * r + 1, :], bias_row).then_inc(biases_in, 16)

            with act.Fori(0, T // 2) as g:
                i = g * 2
                for u in range(2):
                    t = i + u
                    act.wait_ge(diag_cleared, i + (u + 1))
                    act.wait_ge(cands_ready, i + (u + 1))
                    ring = adj_ring[:, bass.ds((i + u) % ADJ_RING, 1)].rearrange("p a n -> p (a n)")
                    af(coded[:, u], ring, ACT.Sign, accum_out=count[:, bass.ds(i + u, 1)]).then_inc(mask_cast, 1)
                    act.wait_ge(kv_product, i + (u + 1))
                    af(kv[:, bass.ds(i + u, 1)].rearrange("p a n -> p (a n)"), bank[u], ACT.Copy).then_inc(kv_stored, 1)
                    act.wait_ge(q_product, i + (u + 1))
                    af(q[:, bass.ds(i + u, 1)].rearrange("p a n -> p (a n)"), bank[2 + u][:, 0:D], ACT.Copy).then_inc(q_stored, 1)
                    act.wait_ge(kv_stored, i + (u + 3))
                    act.dma_start(kv_table[bass.ds((i + u) * P, P), :],
                                  kv[:, bass.ds(i + u, 1)].rearrange("p a n -> p (a n)")).then_inc(table_written, 16)

            def stage_idx(t, u):
                wait(act, gathered[u], (t - u) * (SLOTS * 8))
                src = idx[:, t, 0:SLOTS] if isinstance(t, int) else idx[:, bass.ds(t, 1), 0:SLOTS].rearrange("p a s -> p (a s)")
                af(idx_ring[:, u], src, ACT.Copy).then_inc(idx_staged, 1)

            def ctx_copy(t, u):
                act.wait_ge(ctx_summed, t + 1)
                wait(act, wo_done, t)
                af(ctx_t[:].rearrange("p a b -> p (a b)"), bank[1][:, 0:D], ACT.Copy).then_inc(ctx_copied, 1)

            def relus(t):
                for g in range(FB // 2):
                    act.wait_ge(ff1_ready, 2 * (t - 3) + g + 1)
                    if g == 0:
                        wait(act, ff2_done, t - 3)
                    for j in range(2):
                        f = 2 * g + j
                        last = af(hid[:, f].rearrange("p a b -> p (a b)"), bank[4 + g % 2][:, bass.ts(j, 2 * P)],
                                  ACT.Relu, bias=b1[:, f:f + 1])
                    last.then_inc(relu_done, 1)

            def h1_copy(t, u):
                act.wait_ge(h1_turned, t + 1)
                wait(act, ff1_ready, 2 * (t - u))
                af(h1_t[:, :, u], bank[3][:, 0:D].rearrange("p (k n) -> p k n", k=KD), ACT.Copy).then_inc(h1_copied, 1)

            def post(t, u):
                if on(t, 1):
                    ctx_copy(t - 1, 1 - u)
                if u == 1 and on(t, 3):
                    relus(t)
                if on(t, 1):
                    h1_copy(t - 1, 1 - u)

            def fast():
                act.wait_ge(idx_ready, 1)
                stage_idx(0, 0)
                stage_idx(1, 1)
                act.wait_ge(v_shifted, 1)
                af(ex[:, 0:SLOTS].rearrange("p s h -> p (s h)"), sc[:, 0:SLOTS].rearrange("p s h -> p (s h)"),
                   ACT.Exp, scale=SCALE).then_inc(v_exp, 1)

                def step(t, u):
                    if (isinstance(t, int) and 1 <= t < T - 1) or not isinstance(t, int):
                        stage_idx(t + 1, 1 - u)
                    if on(t, 0):
                        act.wait_ge(shifted, t + 1)
                        af(ex[:].rearrange("p s h -> p (s h)"), sc[:].rearrange("p s h -> p (s h)"),
                           ACT.Exp, scale=SCALE).then_inc(exp_done, 1)
                    post(t, u)

                for t in range(0, LAG + 1):
                    step(t, t % 2)
                with act.Fori((LAG + 1) // 2, (T - 2) // 2) as g:
                    t = g * 2
                    step(t, 0)
                    step(t + 1, 1)
                for t in range(T - 2, T + LAG):
                    step(t, t % 2)

            def dense():
                def step(t, u):
                    if on(t, 0):
                        with act.Fori(0, H) as h:
                            act.wait_ge(d_max, t * H + h + 1)
                            af(d_p, d_sc, ACT.Exp, bias=mx[:, 0:1], scale=SCALE, accum_out=lsum[:, 0:1]).then_inc(d_exp, 1)
                    post(t, u)
                steps(act, step)

            act.wait_ge(late_weights_in, 16 * 8)
            both_ways(act, fast, dense)

        @block.vector
        def _(dve):
            v = nc.vector
            dve.wait_ge(biases_in, 48)
            v.tensor_copy(b_hi, b_raw).then_inc(bias_step, 1)
            dve.wait_ge(bias_step, 1)
            v.tensor_tensor(b_rest, b_raw, b_hi, ALU.subtract).then_inc(bias_step, 1)
            dve.wait_ge(bias_step, 2)
            v.tensor_copy(b_mid, b_rest).then_inc(bias_step, 1)
            dve.wait_ge(bias_step, 3)
            v.tensor_copy(bias_parts[0:32, :], b_hi[0:32]).then_inc(bias_step, 1)
            v.tensor_copy(bias_parts[32:64, :], b_mid[32:64]).then_inc(bias_step, 1)
            v.tensor_tensor(bias_parts[64:96, :], b_rest[64:96], b_mid[64:96], ALU.subtract).then_inc(bias_step, 1)
            dve.wait_ge(bias_step, 6)
            v.memset(small[:, 7, 0:1], 0.0).then_inc(bias_step, 2)
            v.memset(small[:, 7, 1:2], 0.0).then_inc(kv_stored, 2)
            v.memset(small[:, 7, 2:3], 0.0).then_inc(q_stored, 2)
            v.memset(small[:, 7, 3:4], 0.0).then_inc(cands_ready, 2)

            dve.wait_ge(pool_consts, 11)
            with dve.Fori(0, T // 2) as g:
                i = g * 2
                for u in range(2):
                    dve.wait_ge(mask_cast, i + (u + 1))
                    v.tensor_tensor(coded[:, u], coded[:, u], col_no[:], ALU.mult).then_inc(coded_ready, 1)
                for u in range(2):
                    wait_alone(dve, coded_ready, i + (u + 1))
                    for c in range(4):
                        last = v.max(cand[:, u, bass.ts(c, 8)], coded[:, u, bass.ts(c, QUARTER)])
                    last.then_inc(cands_ready, 1)
                for u in range(2):
                    wait_alone(dve, cands_ready, i + (u + 3))
                    v.max(top[:, u, 0:8], cand[:, u]).then_inc(tops_ready, 1)
                for u in range(2):
                    wait_alone(dve, tops_ready, i + (u + 1))
                    v.match_replace(cand_rest[:, u], top[:, u, 0:8], cand[:, u], 0.0).then_inc(rest_ready, 1)
                for u in range(2):
                    wait_alone(dve, rest_ready, i + (u + 1))
                    v.max(top[:, u, 8:16], cand_rest[:, u]).then_inc(listed, 1)
                dve.wait_ge(listed, i + 2)
                v.tensor_copy(lists[:, bass.ds(i, 2), 0:LIST], top[:]).then_inc(lists_done, 1)

            dve.wait_ge(lists_done, T // 2)
            lst = lists[:, :, 0:LIST]
            v.tensor_scalar(idx[:], lst, 0.0, float(FAR), ALU.is_equal, ALU.mult).then_inc(prep, 1)
            v.tensor_scalar(mask[:], lst, 0.0, MASKED, ALU.is_equal, ALU.mult).then_inc(prep, 1)
            v.tensor_scalar(small[:, 0], lists[:, :, SLOTS], 0.0, None, ALU.is_gt).then_inc(prep, 1)
            dve.wait_ge(prep, 5)
            v.scalar_tensor_tensor(out=idx[:], in0=lst, scalar=-1.0, in1=idx[:], op0=ALU.add, op1=ALU.add).then_inc(idx_ready, 1)
            v.tensor_scalar(pv[:, 0, 0, 0:T * LIST].rearrange("p (t s) -> p t s", s=LIST), lst, 0.0, None, ALU.is_gt).then_inc(v_step, 1)
            dve.wait_ge(prep_pe, 1)
            v.tensor_copy(vdata[0:T, 0:P], bank[7][0:T, 0:P]).then_inc(v_step, 1)
            dve.wait_ge(v_step, 1)
            v.tensor_reduce(small[:, 1], pv[:, 0, 0, 0:T * LIST].rearrange("p (t s) -> p t s", s=LIST), AX.X, ALU.add).then_inc(v_step, 1)
            v.tensor_reduce(small[:, 4, 1:2], small[:, 0], AX.X, ALU.add).then_inc(v_step, 1)
            dve.wait_ge(v_step, 3)
            dve.wait_ge(mask_cast, T)
            v.tensor_tensor(small[:, 2], count[:], small[:, 1], ALU.not_equal).then_inc(v_step, 1)
            dve.wait_ge(v_step, 5)
            v.tensor_reduce(small[:, 4, 0:1], small[:, 2], AX.X, ALU.add).then_inc(prep, 1)
            dve.wait_ge(prep_pe, 3)
            v.tensor_scalar(small[0:1, 5, 0:1], bank[5][0:1, 0:1], 0.0, None, ALU.is_gt).then_inc(v_step, 1)
            v.tensor_scalar(small[0:1, 5, 1:2], bank[5][0:1, 1:2], float(P), None, ALU.is_gt).then_inc(v_step, 1)
            dve.wait_ge(v_step, 7)
            v.tensor_tensor(flag_i[:], small[0:1, 5, 0:1], small[0:1, 5, 1:2], ALU.max).then_inc(flag_ready, 1)

            def ln_apply(dst, src, mean, rs, g, half, half_n, done, keep=None):
                v.scalar_tensor_tensor(out=lntmp[:], in0=src, scalar=mean, in1=ln[:, g], op0=ALU.subtract, op1=ALU.mult).then_inc(half, 1)
                dve.wait_ge(half, half_n)
                v.scalar_tensor_tensor(out=dst, in0=lntmp[:], scalar=rs, in1=ln[:, g + 1], op0=ALU.mult, op1=ALU.add).then_inc(done, 1)

            def ln1_pre(t, u):
                dve.wait_ge(wo_done, t + 1)
                dve.wait_ge(xr_in[u], (t - u) * 8 + 16)
                v.tensor_tensor(r1[:, u], bank[2][:, 0:D], xr[:, u], ALU.add).then_inc(r1_ready, 1)
                dve.wait_ge(r1_ready, t + 1)
                v.bn_stats(stats[:, 0], r1[:, u]).then_inc(stats1, 1)
                wait_alone(dve, stats1, t + 1)
                v.bn_aggr(mv1[:, u], stats[:, 0]).then_inc(mv1_ready, 1)

            def keep_row(t):
                return h1keep[:, t % 4] if isinstance(t, int) else h1keep[:, bass.ds(t % 4, 1)].rearrange("p a n -> p (a n)")

            def ln1_post(t, u):
                dve.wait_ge(rstd1_ready, t + 1)
                wait(dve, h1_turned, t - 1)
                ln_apply(h1[:, u], r1[:, u], mv1[:, u, 0:1], rstd1[:, u, 1:2], 0, half1, t + 1, h1_ready)
                dve.wait_ge(h1_ready, t + 1)
                v.tensor_copy(keep_row(t), h1[:, u])

            def ln2_pre(t, u):
                dve.wait_ge(ff2_done, t + 1)
                v.tensor_tensor(r2[:, u], bank[6 + u][:, 0:D], keep_row(t), ALU.add).then_inc(r2_ready, 1)
                dve.wait_ge(r2_ready, t + 1)
                v.bn_stats(stats[:, 1], r2[:, u]).then_inc(stats2, 1)
                wait_alone(dve, stats2, t + 1)
                v.bn_aggr(mv2[:, u], stats[:, 1]).then_inc(mv2_ready, 1)

            def ln2_post(t, u):
                dve.wait_ge(rstd2_ready, t + 1)
                wait(dve, stored[u], (t - u) * 8)
                ln_apply(outs[:, u], r2[:, u], mv2[:, u, 0:1], rstd2[:, u, 1:2], 2, half2, t + 1, out_ready)

            def fast():
                v.scalar_tensor_tensor(out=small[:, 3], in0=bank[6][:, 0:T], scalar=1.0, in1=small[:, 0],
                                       op0=ALU.add, op1=ALU.mult).then_inc(v_step, 1)
                dve.wait_ge(v_step, 8)
                for t in range(T):
                    v.tensor_scalar(onehot[:, t], col_no[:, 0:P], small[:, 3, t:t + 1], None, ALU.is_equal).then_inc(onehots, 1)
                dve.wait_ge(vrows_ready, 1)
                v.tensor_copy(vlist[:], bank[5][:, 0:SLOTS + 1]).then_inc(v_step, 1)
                dve.wait_ge(v_step, 9)
                v.tensor_scalar(vmask[:], vlist[:, 0:SLOTS], 0.0, float(FAR), ALU.is_equal, ALU.mult).then_inc(v_step, 1)
                dve.wait_ge(v_step, 10)
                v.scalar_tensor_tensor(out=vidx[:], in0=vlist[:, 0:SLOTS], scalar=-1.0, in1=vmask[:], op0=ALU.add, op1=ALU.add).then_inc(vidx_ready, 1)
                v.tensor_copy(vq[:], bank[4][:, 0:D]).then_inc(v_step, 1)
                dve.wait_ge(v_step, 11)
                dve.wait_ge(vidx_ready, 1)
                v.tensor_scalar(vmask[:], vlist[:, 0:SLOTS], 0.0, MASKED, ALU.is_equal, ALU.mult).then_inc(v_step, 1)
                dve.wait_ge(v_gathered, 16 * SLOTS)
                v.tensor_tensor(prod[:, 0:SLOTS], gath[:, 1, :, 0:D], vq[:].unsqueeze(1).to_broadcast([P, SLOTS, D]), ALU.mult).then_inc(v_step, 1)
                dve.wait_ge(v_step, 13)
                v.tensor_reduce(sc[:, 0:SLOTS].rearrange("p s h -> p (s h)"),
                                prod[:, 0:SLOTS].rearrange("p s (h d) -> p (s h) d", d=DK), AX.X, ALU.add).then_inc(v_step, 1)
                dve.wait_ge(v_step, 14)
                v.tensor_tensor(sc[:, 0:SLOTS], sc[:, 0:SLOTS], vmask[:].unsqueeze(2).to_broadcast([P, SLOTS, H]), ALU.add).then_inc(v_step, 1)
                dve.wait_ge(v_step, 15)
                v.tensor_reduce(vdata[:, D:D + H], sc[:, 0:SLOTS].rearrange("p s h -> p h s"), AX.X, ALU.max).then_inc(v_step, 1)
                dve.wait_ge(v_step, 16)
                v.tensor_tensor(sc[:, 0:SLOTS], sc[:, 0:SLOTS], vdata[:, D:D + H].unsqueeze(1).to_broadcast([P, SLOTS, H]), ALU.subtract).then_inc(v_shifted, 1)
                v.memset(vdata[:, VCOLS - 1:VCOLS], 1.0).then_inc(v_step, 1)
                dve.wait_ge(v_exp, 1)
                v.tensor_reduce(vdata[:, D + H:D + 2 * H], ex[:, 0:SLOTS].rearrange("p s h -> p h s"), AX.X, ALU.add).then_inc(v_step, 1)
                dve.wait_ge(v_step, 18)
                v.reciprocal(rinv[:], vdata[:, D + H:D + 2 * H]).then_inc(v_step, 1)
                dve.wait_ge(v_step, 19)
                v.tensor_tensor(wts[:, 0:SLOTS], ex[:, 0:SLOTS], rinv[:].unsqueeze(1).to_broadcast([P, SLOTS, H]), ALU.mult).then_inc(v_step, 1)
                dve.wait_ge(v_step, 20)
                v.tensor_tensor(pv[:, 0, 0:SLOTS].rearrange("p s (h d) -> p s h d", d=DK),
                                gath[:, 1, :, D:2 * D].rearrange("p s (h d) -> p s h d", d=DK),
                                wts[:, 0:SLOTS].unsqueeze(3).to_broadcast([P, SLOTS, H, DK]), ALU.mult).then_inc(v_step, 1)
                dve.wait_ge(v_step, 21)
                v.tensor_reduce(vdata[:, 0:D], pv[:, 0, 0:SLOTS].rearrange("p s d -> p d s"), AX.X, ALU.add).then_inc(v_done, 1)

                def turn(t, u):
                    wait(dve, merged, t - 1)
                    src = col_no[:, bass.ts(t, P)] if isinstance(t, int) else col_no[:, bass.ds(t * P, P)]
                    v.tensor_scalar(turned[:, u], src, vlist[:, SLOTS:SLOTS + 1], None, ALU.is_equal).then_inc(turned_ready, 1)

                def tile_of(a, t, *rest):
                    if isinstance(t, int):
                        return a[(slice(None), t) + rest]
                    return a[(slice(None), bass.ds(t, 1)) + rest].rearrange("p a n -> p (a n)")

                turn(0, 0)

                def qk(t, u):
                    dve.wait_ge(gathered[u], (t - u) * (SLOTS * 8) + 16 * SLOTS)
                    qt = tile_of(q, t)
                    v.tensor_tensor(prod[:, SELF], qt, tile_of(kv, t, slice(0, D)), ALU.mult)
                    v.tensor_tensor(prod[:, 0:SLOTS], gath[:, u, :, 0:D], qt.unsqueeze(1).to_broadcast([P, SLOTS, D]), ALU.mult).then_inc(prods_ready, 1)
                    dve.wait_ge(prods_ready, t + 1)
                    v.tensor_reduce(sc[:, 0:SLOTS + 1].rearrange("p s h -> p (s h)"),
                                    prod[:].rearrange("p s (h d) -> p (s h) d", d=DK), AX.X, ALU.add).then_inc(sm_step, 1)

                def softmax_a(t, u):
                    m = bank[0]
                    dve.wait_ge(merged, t + 1)
                    v.tensor_scalar(absent[:], m[:, VCOLS - 1:VCOLS], -MASKED, MASKED, ALU.mult, ALU.add).then_inc(sm_step, 1)
                    dve.wait_ge(sm_step, t * 5 + 1)
                    v.tensor_tensor(sc[:, 0:SLOTS], sc[:, 0:SLOTS],
                                    tile_of(mask, t, slice(0, SLOTS)).unsqueeze(2).to_broadcast([P, SLOTS, H]), ALU.add).then_inc(sm_step, 1)
                    dve.wait_ge(sm_step, t * 5 + 2)
                    v.tensor_scalar(sc[:, VIRT], m[:, D:D + H], absent[:, 0:1], None, ALU.add).then_inc(sm_step, 1)
                    dve.wait_ge(sm_step, t * 5 + 4)
                    v.tensor_reduce(mx[:], sc[:].rearrange("p s h -> p h s"), AX.X, ALU.max).then_inc(sm_step, 1)
                    dve.wait_ge(sm_step, t * 5 + 5)
                    v.tensor_tensor(sc[:], sc[:], mx[:].unsqueeze(1).to_broadcast([P, ALLS, H]), ALU.subtract).then_inc(shifted, 1)

                def softmax_b(t, u):
                    m = bank[0]
                    dve.wait_ge(exp_done, t + 1)
                    v.tensor_tensor(ex[:, VIRT], ex[:, VIRT], m[:, D + H:D + 2 * H], ALU.mult).then_inc(sm_step2, 1)
                    dve.wait_ge(sm_step2, t * 4 + 1)
                    v.tensor_reduce(lsum[:], ex[:].rearrange("p s h -> p h s"), AX.X, ALU.add).then_inc(sm_step2, 1)
                    dve.wait_ge(sm_step2, t * 4 + 2)
                    v.reciprocal(rinv[:], lsum[:]).then_inc(sm_step2, 1)
                    dve.wait_ge(sm_step2, t * 4 + 3)
                    v.tensor_tensor(wts[:], ex[:], rinv[:].unsqueeze(1).to_broadcast([P, ALLS, H]), ALU.mult).then_inc(sm_step2, 1)

                def weigh(t, u):
                    wait(dve, ctx_summed, t - 1)
                    dve.wait_ge(sm_step2, t * 4 + 4)
                    v.tensor_tensor(pv[:, u, VIRT].rearrange("p (h d) -> p h d", d=DK), bank[0][:, 0:D].rearrange("p (h d) -> p h d", d=DK),
                                    wts[:, VIRT].unsqueeze(2).to_broadcast([P, H, DK]), ALU.mult)
                    v.tensor_tensor(pv[:, u, SELF].rearrange("p (h d) -> p h d", d=DK), tile_of(kv, t, slice(D, 2 * D)).rearrange("p (h d) -> p h d", d=DK),
                                    wts[:, SELF].unsqueeze(2).to_broadcast([P, H, DK]), ALU.mult)
                    v.tensor_tensor(pv[:, u, 0:SLOTS].rearrange("p s (h d) -> p s h d", d=DK),
                                    gath[:, u, :, D:2 * D].rearrange("p s (h d) -> p s h d", d=DK),
                                    wts[:, 0:SLOTS].unsqueeze(3).to_broadcast([P, SLOTS, H, DK]), ALU.mult).then_inc(pv_ready, 1)

                def step(t, u):
                    if not isinstance(t, int) or t < T - 1:
                        turn(t + 1, 1 - u)
                    if on(t, 0):
                        qk(t, u)
                        softmax_a(t, u)
                    if on(t, 1):
                        ln1_pre(t - 1, 1 - u)
                    if on(t, 0):
                        softmax_b(t, u)
                    if on(t, LAG):
                        ln2_pre(t - LAG, 1 - u)
                    if on(t, 0):
                        weigh(t, u)
                    if on(t, 1):
                        ln1_post(t - 1, 1 - u)
                    if on(t, LAG):
                        ln2_post(t - LAG, 1 - u)

                for t in range(0, LAG + 1):
                    step(t, t % 2)
                with dve.Fori((LAG + 1) // 2, (T - 2) // 2) as g:
                    t = g * 2
                    step(t, 0)
                    step(t + 1, 1)
                for t in range(T - 2, T + LAG):
                    step(t, t % 2)

            def dense():
                v.memset(pv[:].rearrange("p u s d -> p (u s d)"), 0.0).then_inc(v_step, 1)
                dve.wait_ge(v_step, 8)

                def attend(t, u):
                    dve.wait_ge(dense_adj_in, t * 16 + 16)
                    v.tensor_scalar(d_mask, adj_ring[:, 0], 0.0, MASKED, ALU.is_equal, ALU.mult).then_inc(d_mask_step, 1)
                    dve.wait_ge(d_mask_step, t * 2 + 1)
                    blk = d_mask[:, bass.ds(t * P, P)]
                    v.tensor_tensor(blk, blk, not_eye[:], ALU.mult).then_inc(d_mask_step, 1)
                    wait_alone(dve, d_mask_step, t * 2 + 2)
                    if not isinstance(t, int) or t > 1:
                        wait_alone(dve, ctx_summed, t - 1)
                    with dve.Fori(0, H) as h:
                        n = t * H + h
                        k0, m0 = n * 10, n * 14
                        v.tensor_copy(d_k, kv[:, :, bass.ds(h * DK, DK)])
                        qh = q[:, bass.ds(t, 1), bass.ds(h * DK, DK)].rearrange("p a n -> p (a n)")
                        v.tensor_copy(d_q, qh).then_inc(d_staged, 1)
                        dve.wait_ge(d_product, m0 + 1)
                        v.tensor_copy(d_qt, bank[1][0:DK, 0:P]).then_inc(d_staged, 1)
                        for c in range(4):
                            dve.wait_ge(d_product, m0 + 2 + 2 * c)
                            v.tensor_copy(d_t[0:DK], bank[1][0:DK]).then_inc(d_staged, 1)
                            dve.wait_ge(d_product, m0 + 3 + 2 * c)
                            last = v.tensor_tensor(d_sc[:, bass.ts(c, 512)], bank[0], d_mask[:, bass.ts(c, 512)], ALU.add)
                        last.then_inc(d_inv, 1)
                        dve.wait_ge(d_inv, n * 3 + 1)
                        v.tensor_reduce(rinv[:, 0:1], d_sc, AX.X, ALU.max).then_inc(d_inv, 1)
                        dve.wait_ge(d_inv, n * 3 + 2)
                        v.tensor_scalar(mx[:, 0:1], rinv[:, 0:1], -SCALE, None, ALU.mult).then_inc(d_max, 1)
                        dve.wait_ge(d_exp, n + 1)
                        v.reciprocal(rinv[:, 1:2], lsum[:, 0:1]).then_inc(d_inv, 1)
                        for c in range(4):
                            dve.wait_ge(d_product, m0 + 10 + c)
                            v.tensor_copy(d_t, bank[1]).then_inc(d_staged, 1)
                        dve.wait_ge(d_product, m0 + 14)
                        dve.wait_ge(d_inv, n * 3 + 3)
                        v.tensor_scalar(pv[:, u, 0, bass.ds(h * DK, DK)], bank[0][:, 0:DK], rinv[:, 1:2], None, ALU.mult).then_inc(d_done, 1)
                    dve.wait_ge(d_done, t * H + H)
                    v.memset(absent[:], 0.0).then_inc(pv_ready, 1)

                def step(t, u):
                    if on(t, 0):
                        attend(t, u)
                    if on(t, 1):
                        ln1_pre(t - 1, 1 - u)
                    if on(t, LAG):
                        ln2_pre(t - LAG, 1 - u)
                    if on(t, 1):
                        ln1_post(t - 1, 1 - u)
                    if on(t, LAG):
                        ln2_post(t - LAG, 1 - u)
                steps(dve, step)

            dve.wait_ge(late_weights_in, 16 * 8)
            dve.wait_ge(q_stored, T + 2)
            dve.wait_ge(kv_stored, T + 2)
            both_ways(dve, fast, dense)


def kernel(**inputs):
    import numpy as np
    import concourse.bacc as bacc
    from concourse import mybir as mb
    from concourse.bass_utils import run_bass_kernel_spmd

    a = {k.removeprefix("L0_gnn_"): np.asarray(v) for k, v in inputs.items()}
    x = a["x"]
    laid = {
        "x": x,
        "x_t": x.reshape(16, 128, 2, 128).transpose(0, 3, 2, 1).reshape(16, 128, 256),
        "adj": a["adj"],
        "w_kvq": np.concatenate([a["Wk"].T, a["Wv"].T, a["Wq"].T], axis=1),
        "bias_row": np.concatenate([a["bk"], a["bv"], a["bq"], a["bo"], a["b2"]])[None, :],
        "w_o": a["Wo"].T,
        "w_1": a["W1"].T,
        "b_1": a["b1"].reshape(8, 128).T,
        "w_2": a["W2"].T,
        "ln_rows": np.stack([a["ln1_g"], a["ln1_b"], a["ln2_g"], a["ln2_b"]]),
    }
    nc = bacc.Bacc("TRN2", target_bir_lowering=False, num_devices=1)
    arrays, args = {}, []
    for name, v in laid.items():
        v = np.ascontiguousarray(v)
        arrays[f"in_{name}_dram"] = v
        args.append(nc.dram_tensor(f"in_{name}_dram", v.shape, mb.dt.from_np(v.dtype), kind="ExternalInput").ap())
    out = nc.dram_tensor("out_0_dram", (2048, 256), mb.dt.float32, kind="ExternalOutput").ap()
    build(nc, *args, out)
    r = run_bass_kernel_spmd(nc, [arrays], core_ids=[0])
    return r.results[0]["out_0_dram"]
```

```python
from contextlib import ExitStack

import concourse.bass as bass
from concourse import mybir

F32 = mybir.dt.float32
F16 = mybir.dt.float16
BF16 = mybir.dt.bfloat16
I32 = mybir.dt.int32
ALU = mybir.AluOpType
ACT = mybir.ActivationFunctionType
AX = mybir.AxisListType

P = 128
N = 2048
D = 256
H = 8
DK = D // H
FF = 1024
T = N // P
KD = D // P
FB = FF // P
SLOTS = 8
LIST = 16
QUARTER = N // 4
SELF = SLOTS
VIRT = SLOTS + 1
ALLS = SLOTS + 2
SCALE = 1.0 / float(DK) ** 0.5
EPS = 1e-5
MASKED = -1e30
VCOLS = D + 2 * H + 1
BIAS = 5 * D
ADJ_RING = 4
CODE_RING = 4
LAG = 5
OUT_LAG = 6


def build(nc, x, x_t, adj, w_kvq, bias_row, w_o, w_1, b_1, w_2, ln_rows, ln1_columns, out):
    kv_table = nc.dram_tensor("kv_table", (N, 2 * D), F32).ap()
    with ExitStack() as ctx:
        def sb(name, shape, dt=F32):
            return ctx.enter_context(nc.sbuf_tensor(name, shape, dt))

        def sem(name):
            return ctx.enter_context(nc.semaphore(name))

        wkvq = sb("wkvq", [P, KD, 3 * D])
        wo = sb("wo", [P, KD, D])
        w1 = sb("w1", [P, KD, FF])
        w2 = sb("w2", [P, FB, D])
        b1 = sb("b1", [P, FB])
        ln = sb("ln", [P, 4, D])
        bias_parts = sb("bias_parts", [96, BIAS], BF16)
        ones_bf = sb("ones_bf", [P, P], BF16)
        ones = sb("ones", [P, P])
        eye = sb("eye", [P, P])
        not_eye_i = sb("not_eye_i", [P, P], I32)
        not_eye = sb("not_eye", [P, P])
        before = sb("before", [P, P])
        col_no = sb("col_no", [P, N], F16)
        minus_half = sb("minus_half", [P, 1])
        table_end = sb("table_end", [P, 1])
        kv = sb("kv", [P, T, 2 * D])
        q = sb("q", [P, T, D])
        lists = sb("lists", [P, T, LIST + 1], F16)
        mask = sb("mask", [P, T, SLOTS])
        count = sb("count", [P, T])
        xt = sb("xt", [P, ADJ_RING, KD, P])
        adj_ring = sb("adj_ring", [P, ADJ_RING, N], I32)
        cand = sb("cand", [P, 2, 32], F16)
        cand_rest = sb("cand_rest", [P, 2, 32], F16)
        top = sb("top", [P, 2, LIST], F16)
        gath = sb("gath", [P, 2, SLOTS, 2 * D])
        idx_ring = sb("idx_ring", [P, 2, SLOTS], I32)
        prod = sb("prod", [P, SLOTS + 1, D])
        pv = sb("pv", [P, 2, ALLS, D])
        sc = sb("sc", [P, 2, ALLS, H])
        ex = sb("ex", [P, ALLS, H])
        wts = sb("wts", [P, ALLS, H])
        mx = sb("mx", [P, H])
        lsum = sb("lsum", [P, H])
        rinv = sb("rinv", [P, H])
        absent = sb("absent", [P, 1])
        turned = sb("turned", [P, 2, P])
        vdata = sb("vdata", [P, VCOLS])
        vlist = sb("vlist", [P, SLOTS + 1])
        vq = sb("vq", [P, D])
        vidx = sb("vidx", [P, SLOTS], I32)
        vmask = sb("vmask", [P, SLOTS])
        small = sb("small", [P, 8, T])
        flag_i = sb("flag_i", [1, 1], I32)
        ctx_t = sb("ctx_t", [P, KD, P])
        xr = sb("xr", [P, 2, D])
        lntmp = sb("lntmp", [P, D])
        xn = sb("xn", [P, 2, D])
        hid = sb("hid", [P, FB, 2, P])
        ln1_cols = sb("ln1_cols", [P, 2 * KD])
        h1_t = sb("h1_t", [P, KD, 2, P])
        stats = sb("stats", [P, 2, 6])
        mv1 = sb("mv1", [P, 2, 2])
        mv2 = sb("mv2", [P, 2, 2])
        rstd1 = sb("rstd1", [P, 2, 2])
        rstd2 = sb("rstd2", [P, 2, 2])
        coded = pv[:].rearrange("p u s d -> p (u s d)")[:, 0:CODE_RING * N // 2].bitcast(F16).rearrange("p (r n) -> p r n", n=N)
        onehot16 = adj_ring[:, 0, 0:N // 2].bitcast(F16).rearrange("p (t n) -> p t n", t=T)
        onehot = adj_ring[:, 1].bitcast(F32).rearrange("p (t n) -> p t n", t=T)
        gath_v = adj_ring[:, 2:4].rearrange("p a n -> p (a n)").bitcast(F32).rearrange("p (s d) -> p s d", s=SLOTS)
        h1keep = xt[:].rearrange("p r k n -> p r (k n)")
        spent = wkvq[:].rearrange("p k n -> p (k n)").rearrange("p (a u d) -> p a u d", a=3, u=2)
        r1, r2, outs = spent[:, 0], spent[:, 1], spent[:, 2]
        raw = gath[:, 0].rearrange("p s d -> p (s d)")
        b_raw = raw[0:96, 0:BIAS]
        b_rest = raw[0:96, BIAS:2 * BIAS]
        b_hi = raw[0:96, 2 * BIAS:2 * BIAS + BIAS // 2].bitcast(BF16)
        b_mid = raw[0:96, 2 * BIAS + BIAS // 2:3 * BIAS].bitcast(BF16)
        d_mask = adj_ring[:, 1].bitcast(F32)
        d_sc = adj_ring[:, 2].bitcast(F32)
        d_p = adj_ring[:, 3].bitcast(F32)
        d_k = prod[:, 0:2, :].rearrange("p a (b d) -> p (a b) d", d=DK)
        d_q = prod[:, 2, 0:DK]
        d_qt = prod[0:DK, 3, 0:P]
        d_t = prod[:, 4:6, :].rearrange("p a b -> p (a b)")

        psum = ctx.enter_context(nc.psum_tensor("psum", [P, 8, 512], F32))
        bank = [psum[:, b] for b in range(8)]

        weights_in = sem("weights_in")
        biases_in = sem("biases_in")
        late_weights_in = sem("late_weights_in")
        xt_in = [sem(f"xt_in{i}") for i in range(ADJ_RING)]
        adj_in = [sem(f"adj_in{i}") for i in range(ADJ_RING)]
        xr_in = [sem(f"xr_in{i}") for i in range(2)]
        gathered = [sem(f"gathered{i}") for i in range(2)]
        v_gathered = sem("v_gathered")
        dense_adj_in = sem("dense_adj_in")
        bias_zeroed = sem("bias_zeroed")
        pool_consts = sem("pool_consts")
        bias_step = sem("bias_step")
        kv_product = sem("kv_product")
        q_product = sem("q_product")
        kv_stored = sem("kv_stored")
        q_stored = sem("q_stored")
        table_written = sem("table_written")
        diag_cleared = sem("diag_cleared")
        mask_cast = sem("mask_cast")
        coded_ready = sem("coded_ready")
        cands_ready = sem("cands_ready")
        tops_ready = sem("tops_ready")
        rest_ready = sem("rest_ready")
        listed = sem("listed")
        lists_done = sem("lists_done")
        gath_zeroed = sem("gath_zeroed")
        gath_v_zeroed = sem("gath_v_zeroed")
        overflow_marked = sem("overflow_marked")
        totals_summed = sem("totals_summed")
        totals_copied = sem("totals_copied")
        places_summed = sem("places_summed")
        place_ready = sem("place_ready")
        onehot16_ready = sem("onehot16_ready")
        onehot_ready = sem("onehot_ready")
        listed_count = sem("listed_count")
        misses_ready = sem("misses_ready")
        misses_summed = sem("misses_summed")
        flag_ready = sem("flag_ready")
        idx_staged = sem("idx_staged")
        vlist_product = sem("vlist_product")
        vq_product = sem("vq_product")
        vidx_ready = sem("vidx_ready")
        v_step = sem("v_step")
        v_shifted = sem("v_shifted")
        v_exp = sem("v_exp")
        v_done = sem("v_done")
        turned_ready = sem("turned_ready")
        merged = sem("merged")
        prods_ready = sem("prods_ready")
        scores_ready = sem("scores_ready")
        absent_ready = sem("absent_ready")
        masked_scores = sem("masked_scores")
        max_ready = sem("max_ready")
        shifted = sem("shifted")
        exp_done = sem("exp_done")
        virtual_scaled = sem("virtual_scaled")
        sums_ready = sem("sums_ready")
        inverse_ready = sem("inverse_ready")
        weights_ready = sem("weights_ready")
        pv_ready = sem("pv_ready")
        ctx_summed = sem("ctx_summed")
        ctx_copied = sem("ctx_copied")
        wo_done = sem("wo_done")
        r1_ready = sem("r1_ready")
        stats1 = sem("stats1")
        mv1_ready = sem("mv1_ready")
        var1_ready = sem("var1_ready")
        rstd1_ready = sem("rstd1_ready")
        normed = sem("normed")
        h1_scaled = sem("h1_scaled")
        h1_kept = sem("h1_kept")
        h1_turned = sem("h1_turned")
        h1_copied = sem("h1_copied")
        ff1_ready = sem("ff1_ready")
        relu_done = sem("relu_done")
        ff2_done = sem("ff2_done")
        r2_ready = sem("r2_ready")
        stats2 = sem("stats2")
        mv2_ready = sem("mv2_ready")
        var2_ready = sem("var2_ready")
        rstd2_ready = sem("rstd2_ready")
        half2 = sem("half2")
        out_ready = sem("out_ready")
        stored = [sem(f"stored{i}") for i in range(2)]
        d_mask_step = sem("d_mask_step")
        d_staged = sem("d_staged")
        d_product = sem("d_product")
        d_max = sem("d_max")
        d_exp = sem("d_exp")
        d_inv = sem("d_inv")
        d_done = sem("d_done")
        passed = sem("passed")

        block = ctx.enter_context(nc.Block())

        def wait(eng, s, value):
            if not isinstance(value, int) or value > 0:
                eng.wait_ge(s, value)

        def wait_alone(eng, s, value):
            eng.wait_ge(s, value)
            eng.sem_inc(passed, 1)

        def steps(eng, step):
            for t in range(0, OUT_LAG):
                step(t, t % 2)
            with eng.Fori(OUT_LAG // 2, T // 2) as g:
                t = g * 2
                step(t, 0)
                step(t + 1, 1)
            for t in range(T, T + OUT_LAG):
                step(t, t % 2)

        def on(t, lag):
            return not isinstance(t, int) or 0 <= t - lag < T

        def both_ways(eng, fast, dense):
            eng.wait_ge(flag_ready, 1)
            flag = eng.value_load(flag_i[0:1, 0:1], min_val=0, max_val=1)
            with eng.If(flag < 1):
                fast()
            with eng.Else():
                dense()

        @block.sync
        def _(sp):
            sp.dma_start(wkvq[:], w_kvq.rearrange("(k p) n -> p k n", p=P)).then_inc(weights_in, 16)
            for r in range(ADJ_RING):
                sp.dma_start(adj_ring[:, r], adj[bass.ts(r, P), :]).then_inc(adj_in[r], 16)
                sp.dma_start(xt[:, r], x_t[r].rearrange("p (k n) -> p k n", k=KD)).then_inc(xt_in[r], 16)
            with sp.Fori(1, T // ADJ_RING) as g:
                i = g * ADJ_RING
                for r in range(ADJ_RING):
                    sp.wait_ge(mask_cast, i + (r + 1 - ADJ_RING))
                    sp.dma_start(adj_ring[:, r], adj[bass.ds((i + r) * P, P), :]).then_inc(adj_in[r], 16)
                    sp.wait_ge(q_product, i + (r + 1 - ADJ_RING))
                    sp.dma_start(xt[:, r], x_t[bass.ds(i + r, 1)].rearrange("t p (k n) -> p (t k) n", k=KD)).then_inc(xt_in[r], 16)
            sp.dma_start(wo[:], w_o.rearrange("(k p) n -> p k n", p=P)).then_inc(late_weights_in, 16)
            sp.dma_start(w1[:], w_1.rearrange("(k p) n -> p k n", p=P)).then_inc(late_weights_in, 16)
            sp.dma_start(w2[:], w_2.rearrange("(k p) n -> p k n", p=P)).then_inc(late_weights_in, 16)
            sp.dma_start(b1[:], b_1).then_inc(late_weights_in, 16)
            sp.dma_start(ln1_cols[:], ln1_columns).then_inc(late_weights_in, 16)
            for r in range(4):
                sp.dma_start(ln[:, r], ln_rows[r:r + 1, :].to_broadcast([P, D])).then_inc(late_weights_in, 16)

            def step(t, u, dense):
                if on(t, 0):
                    wait(sp, r1_ready, t - 1)
                    sp.dma_start(xr[:, u], x[bass.ds(t * P, P), :]).then_inc(xr_in[u], 16)
                    if dense:
                        if isinstance(t, int) and t == 0:
                            sp.wait_ge(vlist_product, 1)
                        wait(sp, d_mask_step, 2 * t)
                        sp.dma_start(adj_ring[:, 0], adj[bass.ds(t * P, P), :]).then_inc(dense_adj_in, 16)
                if on(t, OUT_LAG):
                    sp.wait_ge(out_ready, t - (OUT_LAG - 1))
                    sp.dma_start(out[bass.ds((t - OUT_LAG) * P, P), :], outs[:, u]).then_inc(stored[u], 16)

            both_ways(sp, lambda: steps(sp, lambda t, u: step(t, u, False)),
                      lambda: steps(sp, lambda t, u: step(t, u, True)))
            for u in range(2):
                sp.wait_ge(stored[u], 16 * T // 2)

        @block.gpsimd
        def _(pool):
            nc.gpsimd.memset(b_raw, 0.0).then_inc(bias_zeroed, 1)
            nc.gpsimd.memset(not_eye_i[:], 1).then_inc(pool_consts, 1)
            nc.gpsimd.memset(ones[:], 1.0).then_inc(pool_consts, 1)
            nc.gpsimd.memset(ones_bf[:], 1.0).then_inc(pool_consts, 1)
            nc.gpsimd.memset(eye[:], 0.0).then_inc(pool_consts, 1)
            nc.gpsimd.memset(minus_half[:], -0.5).then_inc(pool_consts, 1)
            nc.gpsimd.memset(table_end[:], float(N)).then_inc(pool_consts, 1)
            nc.gpsimd.iota(lists[:, :, LIST], [[-P, T]], base=N, channel_multiplier=-1,
                           allow_small_or_imprecise_dtypes=True).then_inc(pool_consts, 1)
            pool.wait_ge(pool_consts, 7)
            nc.gpsimd.affine_select(out=not_eye_i[:], in_=not_eye_i[:], compare_op=ALU.not_equal, fill=0.0,
                                    base=0, pattern=[[-1, P]], channel_multiplier=1).then_inc(pool_consts, 1)
            nc.gpsimd.iota(col_no[:], [[-1, N]], base=N, channel_multiplier=0,
                           allow_small_or_imprecise_dtypes=True).then_inc(pool_consts, 1)
            nc.gpsimd.affine_select(out=not_eye[:], in_=ones[:], compare_op=ALU.not_equal, fill=0.0,
                                    base=0, pattern=[[-1, P]], channel_multiplier=1).then_inc(pool_consts, 1)
            nc.gpsimd.affine_select(out=eye[:], in_=eye[:], compare_op=ALU.not_equal, fill=1.0,
                                    base=0, pattern=[[-1, P]], channel_multiplier=1).then_inc(pool_consts, 1)
            nc.gpsimd.affine_select(out=before[:], in_=ones[:], compare_op=ALU.is_gt, fill=0.0,
                                    base=0, pattern=[[1, P]], channel_multiplier=-1).then_inc(pool_consts, 1)
            pool.wait_ge(pool_consts, 12)
            def clear_diagonal(i, r):
                pool.wait_ge(adj_in[r], i * (16 // ADJ_RING) + 16)
                blk = adj_ring[:, r, bass.ds((i + r) * P, P)]
                nc.gpsimd.tensor_tensor(blk, blk, not_eye_i[:], ALU.mult).then_inc(diag_cleared, 1)

            for r in range(ADJ_RING):
                clear_diagonal(0, r)
            pool.wait_ge(bias_step, 6)
            nc.gpsimd.memset(gath[:].rearrange("p u s d -> p (u s d)"), 0.0).then_inc(gath_zeroed, 1)
            with pool.Fori(1, T // ADJ_RING) as g:
                for r in range(ADJ_RING):
                    clear_diagonal(g * ADJ_RING, r)
            for h in range(2):
                pool.wait_ge(mask_cast, T - 1 + h)
                nc.gpsimd.memset(adj_ring[:, 2 + h].bitcast(F32), 0.0).then_inc(gath_v_zeroed, 1)
            pool.wait_ge(table_written, 16 * T)
            pool.wait_ge(gath_zeroed, 1)

            def rows_of(ix, dst, done, slots=range(SLOTS)):
                for s in slots:
                    pool.indirect_dma_start(dst[:, s, :], None, kv_table,
                                            bass.IndirectOffsetOnAxis(ap=ix[:, s:s + 1], axis=0),
                                            bounds_check=N - 1, oob_is_err=False).then_inc(done, 16)

            def gather(t, u):
                wait_alone(pool, idx_staged, t + 1)
                if not isinstance(t, int) or t > 1:
                    wait_alone(pool, pv_ready, t - 1)
                rows_of(idx_ring[:, u], gath[:, u], gathered[u])

            def rstd(t, u, mv, res, mv_sem, var_sem, res_sem):
                wait_alone(pool, mv_sem, t + 1)
                nc.gpsimd.tensor_scalar(res[:, u, 0:1], mv[:, u, 1:2], EPS, None, ALU.add).then_inc(var_sem, 1)
                pool.wait_ge(var_sem, t + 1)
                nc.gpsimd.tensor_tensor(res[:, u, 1:2], res[:, u, 0:1], minus_half[:], ALU.pow).then_inc(res_sem, 1)

            def keep(t, u):
                row = h1keep[:, t % 4] if isinstance(t, int) else h1keep[:, bass.ds(t % 4, 1)].rearrange("p a n -> p (a n)")
                if not isinstance(t, int) or t > 3:
                    wait_alone(pool, r2_ready, t - 3)
                wait_alone(pool, normed, t + 1)
                nc.gpsimd.tensor_tensor(row, xn[:, u], ln[:, 0], ALU.mult).then_inc(h1_scaled, 1)
                wait_alone(pool, h1_scaled, t + 1)
                nc.gpsimd.tensor_tensor(row, row, ln[:, 1], ALU.add).then_inc(h1_kept, 1)

            def step(t, u, dense):
                if not dense and (not isinstance(t, int) or 1 <= t < T - 1):
                    gather(t + 1, 1 - u)
                if on(t, 2):
                    keep(t - 2, u)
                if on(t, 1):
                    rstd(t - 1, 1 - u, mv1, rstd1, mv1_ready, var1_ready, rstd1_ready)
                if on(t, LAG):
                    rstd(t - LAG, 1 - u, mv2, rstd2, mv2_ready, var2_ready, rstd2_ready)

            gather(0, 0)
            wait_alone(pool, idx_staged, 2)
            rows_of(idx_ring[:, 1], gath[:, 1], gathered[1], range(SLOTS // 2))
            pool.wait_ge(gath_v_zeroed, 2)
            pool.wait_ge(vidx_ready, 1)
            rows_of(vidx[:], gath_v, v_gathered)
            rows_of(idx_ring[:, 1], gath[:, 1], gathered[1], range(SLOTS // 2, SLOTS))

            def fast():
                for t in range(0, OUT_LAG):
                    step(t, t % 2, False)
                with pool.Fori(OUT_LAG // 2, (T - 2) // 2) as g:
                    t = g * 2
                    step(t, 0, False)
                    step(t + 1, 1, False)
                for t in range(T - 2, T + OUT_LAG):
                    step(t, t % 2, False)

            both_ways(pool, fast, lambda: steps(pool, lambda t, u: step(t, u, True)))

        @block.tensor
        def _(pe):
            mm, tr = nc.tensor.matmul, nc.tensor.transpose

            def bias(dst, first, at):
                mm(dst, ones_bf[0:96, :], bias_parts[:, at:at + dst.shape[-1]], start=first, stop=False)

            pe.wait_ge(weights_in, 16)
            pe.wait_ge(pool_consts, 12)
            pe.wait_ge(bias_step, 6)
            with pe.Fori(0, T // ADJ_RING) as g:
                i = g * ADJ_RING
                for r in range(ADJ_RING):
                    b = r % 2
                    pe.wait_ge(xt_in[r], i * (16 // ADJ_RING) + 16)
                    pe.wait_ge(kv_stored, i + (r + 1))
                    bias(bank[b], True, 0)
                    for k in range(KD):
                        last = mm(bank[b], xt[:, r, k], wkvq[:, k, 0:2 * D], start=False, stop=k == KD - 1)
                    last.then_inc(kv_product, 1)
                    pe.wait_ge(q_stored, i + (r + 1))
                    bias(bank[2 + b][:, 0:D], True, 2 * D)
                    for k in range(KD):
                        last = mm(bank[2 + b][:, 0:D], xt[:, r, k], wkvq[:, k, 2 * D:3 * D], start=False, stop=k == KD - 1)
                    last.then_inc(q_product, 1)

            pe.wait_ge(overflow_marked, 1)
            mm(bank[7][0:T, 0:P], small[:, 0], ones[:], start=True, stop=True).then_inc(totals_summed, 1)
            mm(bank[6][:, 0:T], before[:], small[:, 0], start=True, stop=False)
            pe.wait_ge(totals_copied, 1)
            mm(bank[6][:, 0:T], vdata[0:T, 0:P], before[0:T, 0:T], start=False, stop=True).then_inc(places_summed, 1)
            pe.wait_ge(onehot16_ready, 1)
            for t in range(T):
                last = mm(bank[5][:, 0:SLOTS + 1], onehot16[:, t], lists[:, t, SLOTS:LIST + 1], start=t == 0, stop=t == T - 1)
            last.then_inc(vlist_product, 1)
            pe.wait_ge(misses_ready, 2)
            mm(bank[4][0:1, 0:2], ones[:, 0:1], small[:, 4, 0:2], start=True, stop=True).then_inc(misses_summed, 1)

            def post(t, u, first=None):
                if on(t, 1):
                    pe.wait_ge(pv_ready, t)
                    if first and on(t, 0):
                        first(t, u)
                    wait(pe, ctx_copied, t - 1)
                    for k in range(KD):
                        for s in range(ALLS):
                            last = mm(bank[1][:, bass.ts(k, P)], pv[:, 1 - u, s, bass.ts(k, P)], eye[:],
                                      start=k == 0 and s == 0, stop=s == ALLS - 1, skip_group_check=True)
                    last.then_inc(ctx_summed, 1)
                if on(t, 1):
                    pe.wait_ge(ctx_copied, t)
                    wait(pe, r1_ready, t - 1)
                    bias(bank[2][:, 0:D], True, 3 * D)
                    for k in range(KD):
                        last = mm(bank[2][:, 0:D], ctx_t[:, k], wo[:, k], start=False, stop=k == KD - 1)
                    last.then_inc(wo_done, 1)
                if u == 1 and on(t, 3):
                    pe.wait_ge(h1_copied, t - 1)
                    for g in range(FB // 2):
                        wait(pe, relu_done, 2 * (t - 3) + g - 1)
                        for j in range(2):
                            for k in range(KD):
                                f = 2 * g + j
                                last = mm(bank[4 + g % 2][:, bass.ts(j, 2 * P)], w1[:, k, bass.ts(f, P)],
                                          h1_t[:, k].rearrange("p a b -> p (a b)"),
                                          start=k == 0 and j == 0, stop=k == KD - 1, skip_group_check=True)
                        last.then_inc(ff1_ready, 1)
                if u == 0 and on(t, 4):
                    pe.wait_ge(relu_done, 2 * (t - 4) + FB // 2)
                    for v in range(2):
                        wait(pe, r2_ready, t - 5 + v)
                        bias(bank[6 + v][:, 0:D], True, 4 * D)
                        for f in range(FB):
                            last = mm(bank[6 + v][:, 0:D], hid[:, f, v], w2[:, f], start=False, stop=f == FB - 1)
                        last.then_inc(ff2_done, 1)
                if on(t, 1):
                    pe.wait_ge(normed, t)
                    wait(pe, h1_copied, t - 1)
                    for k in range(KD):
                        last = tr(bank[3][:, bass.ts(k, P)], xn[:, 1 - u, bass.ts(k, P)], eye[:])
                    last.then_inc(h1_turned, 1)

            def fetch_virtual(t, u):
                pe.wait_ge(turned_ready, t + 1)
                wait(pe, pv_ready, t)
                mm(bank[0][:, 0:VCOLS], turned[:, u], vdata[:], start=True, stop=True).then_inc(merged, 1)

            def fast():
                pe.wait_ge(onehot_ready, 1)
                for t in range(T):
                    last = mm(bank[4][:, 0:D], onehot[:, t], q[:, t], start=t == 0, stop=t == T - 1)
                last.then_inc(vq_product, 1)
                pe.wait_ge(v_done, 1)
                fetch_virtual(0, 0)

                steps(pe, lambda t, u: post(t, u, fetch_virtual))

            def dense():
                def heads(t):
                    if not isinstance(t, int) or t > 1:
                        wait_alone(pe, ctx_copied, t - 1)
                    with pe.Fori(0, H) as h:
                        n = t * H + h
                        k0, m0 = n * 10, n * 14
                        pe.wait_ge(d_staged, k0 + 1)
                        tr(bank[1][0:DK, 0:P], d_q, eye[:]).then_inc(d_product, 1)
                        for c in range(4):
                            pe.wait_ge(d_staged, k0 + 2 + c)
                            for j in range(4):
                                last = tr(bank[1][0:DK, bass.ts(j, P)], d_k[:, 4 * c + j], eye[:])
                            last.then_inc(d_product, 1)
                            pe.wait_ge(d_staged, k0 + 3 + c)
                            mm(bank[0], d_qt, d_t[0:DK], start=True, stop=True).then_inc(d_product, 1)
                        pe.wait_ge(d_exp, n + 1)
                        for c in range(4):
                            if c:
                                pe.wait_ge(d_staged, k0 + 6 + c)
                            for j in range(4):
                                last = tr(bank[1][:, bass.ts(j, P)], d_p[:, bass.ts(4 * c + j, P)], eye[:])
                            last.then_inc(d_product, 1)
                            pe.wait_ge(d_staged, k0 + 7 + c)
                            for j in range(4):
                                m = 4 * c + j
                                last = mm(bank[0][:, 0:DK], d_t[:, bass.ts(j, P)],
                                          kv[:, m, bass.ds(h * DK + D, DK)], start=m == 0, stop=m == T - 1)
                        last.then_inc(d_product, 1)

                def step(t, u):
                    if on(t, 0):
                        heads(t)
                    post(t, u)
                steps(pe, step)

            pe.wait_ge(late_weights_in, 16 * 9)
            both_ways(pe, fast, dense)

        @block.scalar
        def _(act):
            af = nc.scalar.activation
            act.wait_ge(bias_zeroed, 1)
            for r in range(3):
                act.dma_start(b_raw[32 * r:32 * r + 1, :], bias_row).then_inc(biases_in, 16)

            with act.Fori(0, T // ADJ_RING) as g:
                i = g * ADJ_RING
                for pair in range(0, ADJ_RING, 2):
                    for u in range(2):
                        t, r = i + (pair + u), pair + u
                        act.wait_ge(diag_cleared, t + 1)
                        act.wait_ge(cands_ready, t + 1)
                        af(coded[:, r], adj_ring[:, r], ACT.Sign, accum_out=count[:, bass.ds(t, 1)]).then_inc(mask_cast, 1)
                    for u in range(2):
                        t = i + (pair + u)
                        kv_rows = kv[:, bass.ds(t, 1)].rearrange("p a n -> p (a n)")
                        act.wait_ge(kv_product, t + 1)
                        af(kv_rows, bank[u], ACT.Copy).then_inc(kv_stored, 1)
                        act.wait_ge(q_product, t + 1)
                        af(q[:, bass.ds(t, 1)].rearrange("p a n -> p (a n)"), bank[2 + u][:, 0:D], ACT.Copy).then_inc(q_stored, 1)
                        act.wait_ge(kv_stored, t + 3)
                        act.dma_start(kv_table[bass.ds(t * P, P), :], kv_rows).then_inc(table_written, 16)

            def index(dst, codes, done):
                af(dst, codes, ACT.Identity, bias=table_end[:, 0:1], scale=-1.0).then_inc(done, 1)

            def stage_idx(t, u):
                wait(act, gathered[u], (t - u) * (SLOTS * 8))
                src = lists[:, t, 0:SLOTS] if isinstance(t, int) else lists[:, bass.ds(t, 1), 0:SLOTS].rearrange("p a s -> p (a s)")
                index(idx_ring[:, u], src, idx_staged)

            act.wait_ge(lists_done, 1)
            stage_idx(0, 0)
            stage_idx(1, 1)
            act.wait_ge(vlist_product, 1)
            index(vidx[:], bank[5][:, 0:SLOTS], vidx_ready)

            def ctx_copy(t, u):
                act.wait_ge(ctx_summed, t + 1)
                wait(act, wo_done, t)
                af(ctx_t[:].rearrange("p a b -> p (a b)"), bank[1][:, 0:D], ACT.Copy).then_inc(ctx_copied, 1)

            def relus(t):
                for g in range(FB // 2):
                    act.wait_ge(ff1_ready, 2 * (t - 3) + g + 1)
                    if g == 0:
                        wait(act, ff2_done, t - 3)
                    for j in range(2):
                        f = 2 * g + j
                        last = af(hid[:, f].rearrange("p a b -> p (a b)"), bank[4 + g % 2][:, bass.ts(j, 2 * P)],
                                  ACT.Relu, bias=b1[:, f:f + 1])
                    last.then_inc(relu_done, 1)

            def h1_copy(t, u):
                act.wait_ge(h1_turned, t + 1)
                wait(act, ff1_ready, 2 * (t - u))
                for k in range(KD):
                    last = af(h1_t[:, k, u], bank[3][:, bass.ts(k, P)], ACT.Identity,
                              bias=ln1_cols[:, KD + k:KD + k + 1], scale=ln1_cols[:, k:k + 1])
                last.then_inc(h1_copied, 1)

            def post(t, u):
                if u == 1 and on(t, 3):
                    relus(t)
                if on(t, 1):
                    h1_copy(t - 1, 1 - u)

            def fast():
                act.wait_ge(onehot16_ready, 1)
                af(onehot.rearrange("p t n -> p (t n)"), onehot16.rearrange("p t n -> p (t n)"), ACT.Copy).then_inc(onehot_ready, 1)
                act.wait_ge(v_shifted, 1)
                af(ex[:, 0:SLOTS].rearrange("p s h -> p (s h)"), sc[:, 1, 0:SLOTS].rearrange("p s h -> p (s h)"),
                   ACT.Exp, scale=SCALE).then_inc(v_exp, 1)

                def step(t, u):
                    if on(t, 1):
                        ctx_copy(t - 1, 1 - u)
                    if on(t, 0):
                        act.wait_ge(shifted, t + 1)
                        af(ex[:].rearrange("p s h -> p (s h)"), sc[:, u].rearrange("p s h -> p (s h)"),
                           ACT.Exp, scale=SCALE).then_inc(exp_done, 1)
                    if not isinstance(t, int) or t < T - 2:
                        stage_idx(t + 2, u)
                    post(t, u)

                for t in range(0, OUT_LAG):
                    step(t, t % 2)
                with act.Fori(OUT_LAG // 2, (T - 2) // 2) as g:
                    t = g * 2
                    step(t, 0)
                    step(t + 1, 1)
                for t in range(T - 2, T + OUT_LAG):
                    step(t, t % 2)

            def dense():
                def step(t, u):
                    if on(t, 0):
                        with act.Fori(0, H) as h:
                            act.wait_ge(d_max, t * H + h + 1)
                            af(d_p, d_sc, ACT.Exp, bias=mx[:, 0:1], scale=SCALE, accum_out=lsum[:, 0:1]).then_inc(d_exp, 1)
                    if on(t, 1):
                        ctx_copy(t - 1, 1 - u)
                    post(t, u)
                steps(act, step)

            act.wait_ge(late_weights_in, 16 * 9)
            both_ways(act, fast, dense)

        @block.vector
        def _(dve):
            v = nc.vector
            v.memset(small[:, 7, 1:2], 0.0).then_inc(kv_stored, 2)
            v.memset(small[:, 7, 2:3], 0.0).then_inc(q_stored, 2)
            v.memset(small[:, 7, 3:4], 0.0).then_inc(cands_ready, CODE_RING)
            dve.wait_ge(biases_in, 48)
            v.tensor_copy(b_hi, b_raw).then_inc(bias_step, 1)
            dve.wait_ge(bias_step, 1)
            v.tensor_tensor(b_rest, b_raw, b_hi, ALU.subtract).then_inc(bias_step, 1)
            dve.wait_ge(bias_step, 2)
            v.tensor_copy(b_mid, b_rest).then_inc(bias_step, 1)
            dve.wait_ge(bias_step, 3)
            v.tensor_copy(bias_parts[0:32, :], b_hi[0:32]).then_inc(bias_step, 1)
            v.tensor_copy(bias_parts[32:64, :], b_mid[32:64]).then_inc(bias_step, 1)
            v.tensor_tensor(bias_parts[64:96, :], b_rest[64:96], b_mid[64:96], ALU.subtract).then_inc(bias_step, 1)

            dve.wait_ge(pool_consts, 12)
            with dve.Fori(0, T // CODE_RING) as g:
                for pair in range(0, CODE_RING, 2):
                    i = g * CODE_RING + pair
                    for u in range(2):
                        dve.wait_ge(mask_cast, i + (u + 1))
                        v.tensor_tensor(coded[:, pair + u], coded[:, pair + u], col_no[:], ALU.mult).then_inc(coded_ready, 1)
                    for u in range(2):
                        wait_alone(dve, coded_ready, i + (u + 1))
                        for c in range(4):
                            last = v.max(cand[:, u, bass.ts(c, 8)], coded[:, pair + u, bass.ts(c, QUARTER)])
                        last.then_inc(cands_ready, 1)
                    for u in range(2):
                        wait_alone(dve, cands_ready, i + (u + 1 + CODE_RING))
                        v.max(top[:, u, 0:8], cand[:, u]).then_inc(tops_ready, 1)
                    for u in range(2):
                        wait_alone(dve, tops_ready, i + (u + 1))
                        v.match_replace(cand_rest[:, u], top[:, u, 0:8], cand[:, u], 0.0).then_inc(rest_ready, 1)
                    for u in range(2):
                        wait_alone(dve, rest_ready, i + (u + 1))
                        v.max(top[:, u, 8:16], cand_rest[:, u]).then_inc(listed, 1)
                    dve.wait_ge(listed, i + 2)
                    v.tensor_copy(lists[:, bass.ds(i, 2), 0:LIST], top[:]).then_inc(lists_done, 1)

            dve.wait_ge(lists_done, T // 2)
            v.tensor_scalar(small[:, 0], lists[:, :, SLOTS], 0.0, None, ALU.is_gt).then_inc(overflow_marked, 1)
            v.tensor_scalar(small[:, 6], lists[:, :, SLOTS], 0.0, -1.0, ALU.is_gt, ALU.mult).then_inc(overflow_marked, 1)
            present = prod[:, 0, 0:T * LIST].rearrange("p (t s) -> p t s", s=LIST)
            v.tensor_scalar(present, lists[:, :, 0:LIST], 0.0, None, ALU.is_gt).then_inc(listed_count, 1)
            dve.wait_ge(totals_summed, 1)
            v.tensor_copy(vdata[0:T, 0:P], bank[7][0:T, 0:P]).then_inc(totals_copied, 1)
            dve.wait_ge(listed_count, 1)
            v.tensor_reduce(small[:, 1], present, AX.X, ALU.add).then_inc(listed_count, 1)
            v.tensor_reduce(small[:, 4, 1:2], small[:, 0], AX.X, ALU.add).then_inc(misses_ready, 1)
            dve.wait_ge(places_summed, 1)
            dve.wait_ge(overflow_marked, 2)
            v.scalar_tensor_tensor(out=small[:, 3], in0=bank[6][:, 0:T], scalar=float(N), in1=small[:, 6],
                                   op0=ALU.subtract, op1=ALU.mult).then_inc(place_ready, 1)
            dve.wait_ge(place_ready, 1)
            v.tensor_tensor(onehot16, col_no[:, 0:P].unsqueeze(1).to_broadcast([P, T, P]),
                            small[:, 3].unsqueeze(2).to_broadcast([P, T, P]), ALU.is_equal).then_inc(onehot16_ready, 1)
            dve.wait_ge(listed_count, 2)
            v.tensor_tensor(small[:, 2], count[:], small[:, 1], ALU.not_equal).then_inc(listed_count, 1)
            dve.wait_ge(listed_count, 3)
            v.tensor_reduce(small[:, 4, 0:1], small[:, 2], AX.X, ALU.add).then_inc(misses_ready, 1)
            v.tensor_scalar(mask[:], lists[:, :, 0:SLOTS], 0.0, MASKED, ALU.is_equal, ALU.mult).then_inc(v_step, 1)
            dve.wait_ge(misses_summed, 1)
            v.tensor_scalar(small[0:1, 5, 0:1], bank[4][0:1, 0:1], 0.0, None, ALU.is_gt).then_inc(v_step, 1)
            v.tensor_scalar(small[0:1, 5, 1:2], bank[4][0:1, 1:2], float(P), None, ALU.is_gt).then_inc(v_step, 1)
            dve.wait_ge(v_step, 3)
            v.tensor_tensor(flag_i[:], small[0:1, 5, 0:1], small[0:1, 5, 1:2], ALU.max).then_inc(flag_ready, 1)

            def ln1_add(t, u):
                dve.wait_ge(wo_done, t + 1)
                dve.wait_ge(xr_in[u], (t - u) * 8 + 16)
                v.tensor_tensor(r1[:, u], bank[2][:, 0:D], xr[:, u], ALU.add).then_inc(r1_ready, 1)

            def ln1_stats(t, u):
                dve.wait_ge(r1_ready, t + 1)
                v.bn_stats(stats[:, 0], r1[:, u]).then_inc(stats1, 1)

            def ln1_mean(t, u):
                wait_alone(dve, stats1, t + 1)
                v.bn_aggr(mv1[:, u], stats[:, 0]).then_inc(mv1_ready, 1)

            def ln1_norm(t, u):
                dve.wait_ge(rstd1_ready, t + 1)
                wait(dve, h1_turned, t - 1)
                wait(dve, h1_scaled, t - 1)
                v.tensor_scalar(xn[:, u], r1[:, u], mv1[:, u, 0:1], rstd1[:, u, 1:2], ALU.subtract, ALU.mult).then_inc(normed, 1)

            def ln2_add(t, u):
                row = h1keep[:, t % 4] if isinstance(t, int) else h1keep[:, bass.ds(t % 4, 1)].rearrange("p a n -> p (a n)")
                dve.wait_ge(ff2_done, t + 1)
                dve.wait_ge(h1_kept, t + 1)
                v.tensor_tensor(r2[:, u], bank[6 + u][:, 0:D], row, ALU.add).then_inc(r2_ready, 1)

            def ln2_stats(t, u):
                dve.wait_ge(r2_ready, t + 1)
                v.bn_stats(stats[:, 1], r2[:, u]).then_inc(stats2, 1)

            def ln2_mean(t, u):
                wait_alone(dve, stats2, t + 1)
                v.bn_aggr(mv2[:, u], stats[:, 1]).then_inc(mv2_ready, 1)

            def ln2_half(t, u):
                dve.wait_ge(rstd2_ready, t + 1)
                wait(dve, out_ready, t)
                v.scalar_tensor_tensor(out=lntmp[:], in0=r2[:, u], scalar=mv2[:, u, 0:1], in1=ln[:, 2],
                                       op0=ALU.subtract, op1=ALU.mult).then_inc(half2, 1)

            def ln2_out(t, u):
                wait(dve, stored[u], (t - u) * 8)
                dve.wait_ge(half2, t + 1)
                v.scalar_tensor_tensor(out=outs[:, u], in0=lntmp[:], scalar=rstd2[:, u, 1:2], in1=ln[:, 3],
                                       op0=ALU.mult, op1=ALU.add).then_inc(out_ready, 1)

            def turn(t, u):
                wait(dve, merged, t - 1)
                src = col_no[:, bass.ts(t, P)] if isinstance(t, int) else col_no[:, bass.ds(t * P, P)]
                v.tensor_scalar(turned[:, u], src, vlist[:, SLOTS:SLOTS + 1], None, ALU.is_equal).then_inc(turned_ready, 1)

            def tile_of(a, t, *rest):
                if isinstance(t, int):
                    return a[(slice(None), t) + rest]
                return a[(slice(None), bass.ds(t, 1)) + rest].rearrange("p a n -> p (a n)")

            def products(t, u):
                dve.wait_ge(gathered[u], (t - u) * (SLOTS * 8) + 16 * SLOTS)
                qt = tile_of(q, t)
                v.tensor_tensor(prod[:, SELF], qt, tile_of(kv, t, slice(0, D)), ALU.mult)
                v.tensor_tensor(prod[:, 0:SLOTS], gath[:, u, :, 0:D], qt.unsqueeze(1).to_broadcast([P, SLOTS, D]), ALU.mult).then_inc(prods_ready, 1)

            def scores(t, u):
                dve.wait_ge(prods_ready, t + 1)
                v.tensor_reduce(sc[:, u, 0:SLOTS + 1].rearrange("p s h -> p (s h)"),
                                prod[:].rearrange("p s (h d) -> p (s h) d", d=DK), AX.X, ALU.add).then_inc(scores_ready, 1)

            def virtual_absent(t, u):
                dve.wait_ge(merged, t + 1)
                v.tensor_scalar(absent[:], bank[0][:, VCOLS - 1:VCOLS], -MASKED, MASKED, ALU.mult, ALU.add).then_inc(absent_ready, 1)

            def virtual_max(t, u):
                dve.wait_ge(absent_ready, t + 1)
                v.tensor_scalar(sc[:, u, VIRT], bank[0][:, D:D + H], absent[:, 0:1], None, ALU.add).then_inc(masked_scores, 1)

            def mask_scores(t, u):
                dve.wait_ge(scores_ready, t + 1)
                v.tensor_tensor(sc[:, u, 0:SLOTS], sc[:, u, 0:SLOTS],
                                tile_of(mask, t).unsqueeze(2).to_broadcast([P, SLOTS, H]), ALU.add).then_inc(masked_scores, 1)

            def maximum(t, u):
                dve.wait_ge(masked_scores, t * 2 + 2)
                v.tensor_reduce(mx[:], sc[:, u].rearrange("p s h -> p h s"), AX.X, ALU.max).then_inc(max_ready, 1)

            def shift(t, u):
                dve.wait_ge(max_ready, t + 1)
                v.tensor_tensor(sc[:, u], sc[:, u], mx[:].unsqueeze(1).to_broadcast([P, ALLS, H]), ALU.subtract).then_inc(shifted, 1)

            def virtual_sum(t, u):
                dve.wait_ge(exp_done, t + 1)
                v.tensor_tensor(ex[:, VIRT], ex[:, VIRT], bank[0][:, D + H:D + 2 * H], ALU.mult).then_inc(virtual_scaled, 1)

            def sums(t, u):
                dve.wait_ge(virtual_scaled, t + 1)
                v.tensor_reduce(lsum[:], ex[:].rearrange("p s h -> p h s"), AX.X, ALU.add).then_inc(sums_ready, 1)

            def inverse(t, u):
                dve.wait_ge(sums_ready, t + 1)
                v.reciprocal(rinv[:], lsum[:]).then_inc(inverse_ready, 1)

            def weights(t, u):
                dve.wait_ge(inverse_ready, t + 1)
                v.tensor_tensor(wts[:], ex[:], rinv[:].unsqueeze(1).to_broadcast([P, ALLS, H]), ALU.mult).then_inc(weights_ready, 1)

            def weigh(t, u):
                wait(dve, ctx_summed, t - 1)
                dve.wait_ge(weights_ready, t + 1)
                v.tensor_tensor(pv[:, u, VIRT].rearrange("p (h d) -> p h d", d=DK), bank[0][:, 0:D].rearrange("p (h d) -> p h d", d=DK),
                                wts[:, VIRT].unsqueeze(2).to_broadcast([P, H, DK]), ALU.mult)
                v.tensor_tensor(pv[:, u, SELF].rearrange("p (h d) -> p h d", d=DK), tile_of(kv, t, slice(D, 2 * D)).rearrange("p (h d) -> p h d", d=DK),
                                wts[:, SELF].unsqueeze(2).to_broadcast([P, H, DK]), ALU.mult)
                v.tensor_tensor(pv[:, u, 0:SLOTS].rearrange("p s (h d) -> p s h d", d=DK),
                                gath[:, u, :, D:2 * D].rearrange("p s (h d) -> p s h d", d=DK),
                                wts[:, 0:SLOTS].unsqueeze(3).to_broadcast([P, SLOTS, H, DK]), ALU.mult).then_inc(pv_ready, 1)

            def interleaved(t, u, *stages):
                for lag, piece in stages:
                    if on(t, lag):
                        piece(t - lag, (u + lag) % 2)

            def step(t, u):
                if not isinstance(t, int) or t < T - 1:
                    turn(t + 1, 1 - u)
                if not isinstance(t, int) or 0 < t < T:
                    products(t, u)
                    scores(t, u)
                interleaved(t, u, (0, virtual_absent), (0, mask_scores), (LAG, ln2_add), (0, virtual_max),
                            (LAG, ln2_stats), (0, maximum), (LAG, ln2_mean), (OUT_LAG, ln2_half), (0, shift),
                            (OUT_LAG, ln2_out), (0, virtual_sum), (1, ln1_add), (0, sums), (1, ln1_stats),
                            (0, inverse), (1, ln1_mean), (0, weights), (0, weigh), (1, ln1_norm))

            def fast():
                dve.wait_ge(vidx_ready, 1)
                v.tensor_copy(vlist[:], bank[5][:, 0:SLOTS + 1]).then_inc(v_step, 1)
                dve.wait_ge(v_step, 4)
                v.tensor_scalar(vmask[:], vlist[:, 0:SLOTS], 0.0, MASKED, ALU.is_equal, ALU.mult).then_inc(v_step, 1)
                turn(0, 0)
                dve.wait_ge(vq_product, 1)
                v.tensor_copy(vq[:], bank[4][:, 0:D]).then_inc(v_step, 1)
                products(0, 0)
                scores(0, 0)
                vsc = sc[:, 1, 0:SLOTS]
                dve.wait_ge(v_gathered, 16 * SLOTS)
                dve.wait_ge(v_step, 6)
                dve.wait_ge(scores_ready, 1)
                v.tensor_tensor(prod[:, 0:SLOTS], gath_v[:, :, 0:D], vq[:].unsqueeze(1).to_broadcast([P, SLOTS, D]), ALU.mult).then_inc(v_step, 1)
                dve.wait_ge(v_step, 7)
                v.tensor_reduce(vsc.rearrange("p s h -> p (s h)"),
                                prod[:, 0:SLOTS].rearrange("p s (h d) -> p (s h) d", d=DK), AX.X, ALU.add).then_inc(v_step, 1)
                dve.wait_ge(v_step, 8)
                v.tensor_tensor(vsc, vsc, vmask[:].unsqueeze(2).to_broadcast([P, SLOTS, H]), ALU.add).then_inc(v_step, 1)
                dve.wait_ge(v_step, 9)
                v.tensor_reduce(vdata[:, D:D + H], vsc.rearrange("p s h -> p h s"), AX.X, ALU.max).then_inc(v_step, 1)
                dve.wait_ge(v_step, 10)
                v.tensor_tensor(vsc, vsc, vdata[:, D:D + H].unsqueeze(1).to_broadcast([P, SLOTS, H]), ALU.subtract).then_inc(v_shifted, 1)
                v.memset(vdata[:, VCOLS - 1:VCOLS], 1.0).then_inc(v_step, 1)
                dve.wait_ge(v_exp, 1)
                v.tensor_reduce(vdata[:, D + H:D + 2 * H], ex[:, 0:SLOTS].rearrange("p s h -> p h s"), AX.X, ALU.add).then_inc(v_step, 1)
                dve.wait_ge(v_step, 12)
                v.reciprocal(rinv[:], vdata[:, D + H:D + 2 * H]).then_inc(v_step, 1)
                dve.wait_ge(v_step, 13)
                v.tensor_tensor(wts[:, 0:SLOTS], ex[:, 0:SLOTS], rinv[:].unsqueeze(1).to_broadcast([P, SLOTS, H]), ALU.mult).then_inc(v_step, 1)
                dve.wait_ge(v_step, 14)
                v.tensor_tensor(pv[:, 0, 0:SLOTS].rearrange("p s (h d) -> p s h d", d=DK),
                                gath_v[:, :, D:2 * D].rearrange("p s (h d) -> p s h d", d=DK),
                                wts[:, 0:SLOTS].unsqueeze(3).to_broadcast([P, SLOTS, H, DK]), ALU.mult).then_inc(v_step, 1)
                dve.wait_ge(v_step, 15)
                v.tensor_reduce(vdata[:, 0:D], pv[:, 0, 0:SLOTS].rearrange("p s d -> p d s"), AX.X, ALU.add).then_inc(v_done, 1)

                for t in range(0, OUT_LAG):
                    step(t, t % 2)
                with dve.Fori(OUT_LAG // 2, (T - 2) // 2) as g:
                    t = g * 2
                    step(t, 0)
                    step(t + 1, 1)
                for t in range(T - 2, T + OUT_LAG):
                    step(t, t % 2)

            def dense():
                dve.wait_ge(v_gathered, 16 * SLOTS)
                v.memset(pv[:].rearrange("p u s d -> p (u s d)"), 0.0).then_inc(v_step, 1)
                dve.wait_ge(v_step, 4)

                def attend(t, u):
                    dve.wait_ge(dense_adj_in, t * 16 + 16)
                    v.tensor_scalar(d_mask, adj_ring[:, 0], 0.0, MASKED, ALU.is_equal, ALU.mult).then_inc(d_mask_step, 1)
                    dve.wait_ge(d_mask_step, t * 2 + 1)
                    blk = d_mask[:, bass.ds(t * P, P)]
                    v.tensor_tensor(blk, blk, not_eye[:], ALU.mult).then_inc(d_mask_step, 1)
                    wait_alone(dve, d_mask_step, t * 2 + 2)
                    if not isinstance(t, int) or t > 1:
                        wait_alone(dve, ctx_summed, t - 1)
                    with dve.Fori(0, H) as h:
                        n = t * H + h
                        k0, m0 = n * 10, n * 14
                        v.tensor_copy(d_k, kv[:, :, bass.ds(h * DK, DK)])
                        qh = q[:, bass.ds(t, 1), bass.ds(h * DK, DK)].rearrange("p a n -> p (a n)")
                        v.tensor_copy(d_q, qh).then_inc(d_staged, 1)
                        dve.wait_ge(d_product, m0 + 1)
                        v.tensor_copy(d_qt, bank[1][0:DK, 0:P]).then_inc(d_staged, 1)
                        for c in range(4):
                            dve.wait_ge(d_product, m0 + 2 + 2 * c)
                            v.tensor_copy(d_t[0:DK], bank[1][0:DK]).then_inc(d_staged, 1)
                            dve.wait_ge(d_product, m0 + 3 + 2 * c)
                            last = v.tensor_tensor(d_sc[:, bass.ts(c, 512)], bank[0], d_mask[:, bass.ts(c, 512)], ALU.add)
                        last.then_inc(d_inv, 1)
                        dve.wait_ge(d_inv, n * 3 + 1)
                        v.tensor_reduce(rinv[:, 0:1], d_sc, AX.X, ALU.max).then_inc(d_inv, 1)
                        dve.wait_ge(d_inv, n * 3 + 2)
                        v.tensor_scalar(mx[:, 0:1], rinv[:, 0:1], -SCALE, None, ALU.mult).then_inc(d_max, 1)
                        dve.wait_ge(d_exp, n + 1)
                        v.reciprocal(rinv[:, 1:2], lsum[:, 0:1]).then_inc(d_inv, 1)
                        for c in range(4):
                            dve.wait_ge(d_product, m0 + 10 + c)
                            v.tensor_copy(d_t, bank[1]).then_inc(d_staged, 1)
                        dve.wait_ge(d_product, m0 + 14)
                        dve.wait_ge(d_inv, n * 3 + 3)
                        v.tensor_scalar(pv[:, u, 0, bass.ds(h * DK, DK)], bank[0][:, 0:DK], rinv[:, 1:2], None, ALU.mult).then_inc(d_done, 1)
                    dve.wait_ge(d_done, t * H + H)
                    v.memset(absent[:], 0.0).then_inc(pv_ready, 1)

                def step(t, u):
                    if on(t, 0):
                        attend(t, u)
                    interleaved(t, u, (1, ln1_add), (LAG, ln2_add), (1, ln1_stats), (LAG, ln2_stats), (1, ln1_mean),
                                (LAG, ln2_mean), (OUT_LAG, ln2_half), (OUT_LAG, ln2_out), (1, ln1_norm))
                steps(dve, step)

            dve.wait_ge(late_weights_in, 16 * 9)
            dve.wait_ge(q_stored, T + 2)
            dve.wait_ge(kv_stored, T + 2)
            both_ways(dve, fast, dense)


def kernel(**inputs):
    import numpy as np
    import concourse.bacc as bacc
    from concourse import mybir as mb
    from concourse.bass_utils import run_bass_kernel_spmd

    a = {k.removeprefix("L0_gnn_"): np.asarray(v) for k, v in inputs.items()}
    x = a["x"]
    laid = {
        "x": x,
        "x_t": x.reshape(16, 128, 2, 128).transpose(0, 3, 2, 1).reshape(16, 128, 256),
        "adj": a["adj"],
        "w_kvq": np.concatenate([a["Wk"].T, a["Wv"].T, a["Wq"].T], axis=1),
        "bias_row": np.concatenate([a["bk"], a["bv"], a["bq"], a["bo"], a["b2"]])[None, :],
        "w_o": a["Wo"].T,
        "w_1": a["W1"].T,
        "b_1": a["b1"].reshape(8, 128).T,
        "w_2": a["W2"].T,
        "ln_rows": np.stack([a["ln1_g"], a["ln1_b"], a["ln2_g"], a["ln2_b"]]),
        "ln1_columns": np.concatenate([a["ln1_g"].reshape(2, 128), a["ln1_b"].reshape(2, 128)]).T,
    }
    nc = bacc.Bacc("TRN2", target_bir_lowering=False, num_devices=1)
    arrays, args = {}, []
    for name, v in laid.items():
        v = np.ascontiguousarray(v)
        arrays[f"in_{name}_dram"] = v
        args.append(nc.dram_tensor(f"in_{name}_dram", v.shape, mb.dt.from_np(v.dtype), kind="ExternalInput").ap())
    out = nc.dram_tensor("out_0_dram", (2048, 256), mb.dt.float32, kind="ExternalOutput").ap()
    build(nc, *args, out)
    r = run_bass_kernel_spmd(nc, [arrays], core_ids=[0])
    return r.results[0]["out_0_dram"]
```

```python
from contextlib import ExitStack

import concourse.bass as bass
from concourse import mybir

F32 = mybir.dt.float32
F16 = mybir.dt.float16
BF16 = mybir.dt.bfloat16
I32 = mybir.dt.int32
ALU = mybir.AluOpType
ACT = mybir.ActivationFunctionType
AX = mybir.AxisListType

P = 128
N = 2048
D = 256
H = 8
DK = D // H
FF = 1024
T = N // P
KD = D // P
FB = FF // P
SLOTS = 8
LIST = 16
QUARTER = N // 4
SELF = SLOTS
VIRT = SLOTS + 1
ALLS = SLOTS + 2
SCALE = 1.0 / float(DK) ** 0.5
EPS = 1e-5
MASKED = -1e30
VCOLS = D + 2 * H + 1
BIAS = 5 * D
MERGED = 3
WARM = 3
ADJ_RING = 4
CODE_RING = 4
LAG = 5
OUT_LAG = 6


def build(nc, x, x_t, adj, w_kvq, bias_row, w_o, w_1, b_1, w_2, ln_rows, ln1_columns, out):
    kv_table = nc.dram_tensor("kv_table", (N, 2 * D), F32).ap()
    with ExitStack() as ctx:
        def sb(name, shape, dt=F32):
            return ctx.enter_context(nc.sbuf_tensor(name, shape, dt))

        def sem(name):
            return ctx.enter_context(nc.semaphore(name))

        wkvq = sb("wkvq", [P, KD, 3 * D])
        wo = sb("wo", [P, KD, D])
        w1 = sb("w1", [P, KD, FF])
        w2 = sb("w2", [P, FB, D])
        b1 = sb("b1", [P, FB])
        ln = sb("ln", [P, 4, D])
        bias_parts = sb("bias_parts", [96, BIAS], BF16)
        ones_bf = sb("ones_bf", [P, P], BF16)
        ones = sb("ones", [P, P])
        eye = sb("eye", [P, P])
        not_eye_i = sb("not_eye_i", [P, P], I32)
        not_eye = sb("not_eye", [P, P])
        before = sb("before", [P, P])
        col_no = sb("col_no", [P, N], F16)
        minus_half = sb("minus_half", [P, 2])
        table_end = sb("table_end", [P, 1])
        kv = sb("kv", [P, T, 2 * D])
        q = sb("q", [P, T, D])
        lists = sb("lists", [P, T, LIST + 1], F16)
        mask = sb("mask", [P, T, SLOTS])
        count = sb("count", [P, T])
        xt = sb("xt", [P, ADJ_RING, KD, P])
        adj_ring = sb("adj_ring", [P, ADJ_RING, N], I32)
        cand = sb("cand", [P, CODE_RING, 32], F16)
        cand_rest = sb("cand_rest", [P, 2, 32], F16)
        top = sb("top", [P, 2, LIST], F16)
        gath = sb("gath", [P, 2, SLOTS, 2 * D])
        idx_ring = sb("idx_ring", [P, 2, SLOTS], I32)
        prod = sb("prod", [P, SLOTS + 1, D])
        pv = sb("pv", [P, 2, ALLS, D])
        sc = sb("sc", [P, 2, ALLS, H])
        ex = sb("ex", [P, ALLS, H])
        wts = sb("wts", [P, ALLS, H])
        mx = sb("mx", [P, H])
        lsum = sb("lsum", [P, H])
        rinv = sb("rinv", [P, H])
        absent = sb("absent", [P, 1])
        turned = sb("turned", [P, 2, P])
        vdata = sb("vdata", [P, VCOLS])
        vlist = sb("vlist", [P, SLOTS + 1])
        vq = sb("vq", [P, D])
        vidx = sb("vidx", [P, SLOTS], I32)
        vmask = sb("vmask", [P, SLOTS])
        small = sb("small", [P, 8, T])
        flag_i = sb("flag_i", [1, 1], I32)
        ctx_t = sb("ctx_t", [P, KD, P])
        xr = sb("xr", [P, 2, D])
        lntmp = sb("lntmp", [P, D])
        xn = sb("xn", [P, 2, D])
        hid = sb("hid", [P, FB, 2, P])
        ln1_cols = sb("ln1_cols", [P, 2 * KD])
        h1_t = sb("h1_t", [P, KD, 2, P])
        stats = sb("stats", [P, 2, 6])
        mv = sb("mv", [P, 2, 2, 2])
        var_eps = sb("var_eps", [P, 2, 2])
        rstd = sb("rstd", [P, 2, 2])
        minus_mean = sb("minus_mean", [P, 2])
        shift1 = sb("shift1", [P, 2])
        coded = pv[:].rearrange("p u s d -> p (u s d)")[:, 0:CODE_RING * N // 2].bitcast(F16).rearrange("p (r n) -> p r n", n=N)
        onehot16 = adj_ring[:, 0, 0:N // 2].bitcast(F16).rearrange("p (t n) -> p t n", t=T)
        onehot = adj_ring[:, 1].bitcast(F32).rearrange("p (t n) -> p t n", t=T)
        gath_v = adj_ring[:, 2:4].rearrange("p a n -> p (a n)").bitcast(F32).rearrange("p (s d) -> p s d", s=SLOTS)
        h1keep = xt[:].rearrange("p r k n -> p r (k n)")
        spent = wkvq[:].rearrange("p k n -> p (k n)").rearrange("p (a u d) -> p a u d", a=3, u=2)
        r1, r2, outs = spent[:, 0], spent[:, 1], spent[:, 2]
        raw = gath[:, 0].rearrange("p s d -> p (s d)")
        b_raw = raw[0:96, 0:BIAS]
        b_rest = raw[0:96, BIAS:2 * BIAS]
        b_hi = raw[0:96, 2 * BIAS:2 * BIAS + BIAS // 2].bitcast(BF16)
        b_mid = raw[0:96, 2 * BIAS + BIAS // 2:3 * BIAS].bitcast(BF16)
        d_mask = adj_ring[:, 1].bitcast(F32)
        d_sc = adj_ring[:, 2].bitcast(F32)
        d_p = adj_ring[:, 3].bitcast(F32)
        d_k = prod[:, 0:2, :].rearrange("p a (b d) -> p (a b) d", d=DK)
        d_q = prod[:, 2, 0:DK]
        d_qt = prod[0:DK, 3, 0:P]
        d_t = prod[:, 4:6, :].rearrange("p a b -> p (a b)")

        psum = ctx.enter_context(nc.psum_tensor("psum", [P, 8, 512], F32))
        bank = [psum[:, b] for b in range(8)]

        weights_in = sem("weights_in")
        biases_in = sem("biases_in")
        late_weights_in = sem("late_weights_in")
        ff_weights_in = sem("ff_weights_in")
        xt_in = [sem(f"xt_in{i}") for i in range(ADJ_RING)]
        adj_in = [sem(f"adj_in{i}") for i in range(ADJ_RING)]
        xr_in = [sem(f"xr_in{i}") for i in range(2)]
        gathered = [sem(f"gathered{i}") for i in range(2)]
        v_gathered = sem("v_gathered")
        dense_adj_in = sem("dense_adj_in")
        bias_zeroed = sem("bias_zeroed")
        pool_consts = sem("pool_consts")
        bias_step = sem("bias_step")
        kv_product = sem("kv_product")
        q_product = sem("q_product")
        kv_stored = sem("kv_stored")
        q_stored = sem("q_stored")
        table_written = sem("table_written")
        diag_cleared = sem("diag_cleared")
        mask_cast = sem("mask_cast")
        coded_ready = sem("coded_ready")
        cands_ready = sem("cands_ready")
        tops_ready = sem("tops_ready")
        rest_ready = sem("rest_ready")
        listed = sem("listed")
        lists_done = sem("lists_done")
        gath_zeroed = sem("gath_zeroed")
        gath_v_zeroed = sem("gath_v_zeroed")
        overflow_marked = sem("overflow_marked")
        totals_summed = sem("totals_summed")
        totals_copied = sem("totals_copied")
        places_summed = sem("places_summed")
        place_ready = sem("place_ready")
        onehot16_ready = sem("onehot16_ready")
        onehot_ready = sem("onehot_ready")
        listed_count = sem("listed_count")
        misses_ready = sem("misses_ready")
        misses_summed = sem("misses_summed")
        flag_ready = sem("flag_ready")
        idx_staged = sem("idx_staged")
        vlist_product = sem("vlist_product")
        vq_product = sem("vq_product")
        vidx_ready = sem("vidx_ready")
        v_step = sem("v_step")
        v_shifted = sem("v_shifted")
        v_exp = sem("v_exp")
        v_done = sem("v_done")
        turned_ready = sem("turned_ready")
        merged = sem("merged")
        prods_ready = sem("prods_ready")
        self_product = sem("self_product")
        scores_ready = sem("scores_ready")
        absent_ready = sem("absent_ready")
        masked_scores = sem("masked_scores")
        max_ready = sem("max_ready")
        shifted = sem("shifted")
        exp_done = sem("exp_done")
        virtual_scaled = sem("virtual_scaled")
        sums_ready = sem("sums_ready")
        inverse_ready = sem("inverse_ready")
        weights_ready = sem("weights_ready")
        weighted = sem("weighted")
        self_weighted = sem("self_weighted")
        pv_ready = sem("pv_ready")
        ctx_summed = sem("ctx_summed")
        ctx_copied = sem("ctx_copied")
        wo_done = sem("wo_done")
        r1_ready = sem("r1_ready")
        stats1 = sem("stats1")
        mv1_ready = sem("mv1_ready")
        var_ready = sem("var_ready")
        mean1_negated = sem("mean1_negated")
        rstd_ready = sem("rstd_ready")
        shift1_ready = sem("shift1_ready")
        normed = sem("normed")
        h1_scaled = sem("h1_scaled")
        h1_kept = sem("h1_kept")
        h1_turned = sem("h1_turned")
        h1_copied = sem("h1_copied")
        ff1_ready = sem("ff1_ready")
        relu_done = sem("relu_done")
        ff2_done = sem("ff2_done")
        r2_ready = sem("r2_ready")
        stats2 = sem("stats2")
        mv2_ready = sem("mv2_ready")
        half2 = sem("half2")
        out_ready = sem("out_ready")
        stored = [sem(f"stored{i}") for i in range(2)]
        d_mask_step = sem("d_mask_step")
        d_staged = sem("d_staged")
        d_product = sem("d_product")
        d_max = sem("d_max")
        d_exp = sem("d_exp")
        d_inv = sem("d_inv")
        d_done = sem("d_done")
        passed = sem("passed")

        block = ctx.enter_context(nc.Block())

        def wait(eng, s, value):
            if not isinstance(value, int) or value > 0:
                eng.wait_ge(s, value)

        def wait_alone(eng, s, value):
            eng.wait_ge(s, value)
            eng.sem_inc(passed, 1)

        def steps(eng, step):
            for t in range(0, OUT_LAG):
                step(t, t % 2)
            with eng.Fori(OUT_LAG // 2, T // 2) as g:
                t = g * 2
                step(t, 0)
                step(t + 1, 1)
            for t in range(T, T + OUT_LAG):
                step(t, t % 2)

        def on(t, lag):
            return not isinstance(t, int) or 0 <= t - lag < T

        def both_ways(eng, fast, dense):
            eng.wait_ge(flag_ready, 1)
            flag = eng.value_load(flag_i[0:1, 0:1], min_val=0, max_val=1)
            with eng.If(flag < 1):
                fast()
            with eng.Else():
                dense()

        @block.sync
        def _(sp):
            sp.dma_start(wkvq[:], w_kvq.rearrange("(k p) n -> p k n", p=P)).then_inc(weights_in, 16)
            sp.wait_ge(bias_zeroed, 1)
            for r in range(3):
                sp.dma_start(b_raw[32 * r:32 * r + 1, :], bias_row).then_inc(biases_in, 16)
            for r in range(ADJ_RING):
                sp.dma_start(adj_ring[:, r], adj[bass.ts(r, P), :]).then_inc(adj_in[r], 16)
                sp.dma_start(xt[:, r], x_t[r].rearrange("p (k n) -> p k n", k=KD)).then_inc(xt_in[r], 16)

            def load_x_t(t, r):
                sp.wait_ge(q_product, t + (1 - ADJ_RING))
                sp.dma_start(xt[:, r], x_t[bass.ds(t, 1)].rearrange("t p (k n) -> p (t k) n", k=KD)).then_inc(xt_in[r], 16)

            def load_adj(t, r):
                sp.wait_ge(mask_cast, t + (1 - ADJ_RING))
                sp.dma_start(adj_ring[:, r], adj[bass.ds(t * P, P), :]).then_inc(adj_in[r], 16)

            with sp.Fori(1, T // ADJ_RING - 1) as g:
                for r in range(ADJ_RING):
                    load_adj(g * ADJ_RING + r, r)
                    load_x_t(g * ADJ_RING + r, r)
            for r in range(2):
                load_adj(T - ADJ_RING + r, r)
                load_x_t(T - ADJ_RING + r, r)
            for r in range(2, ADJ_RING):
                load_x_t(T - ADJ_RING + r, r)
            for r in range(2, ADJ_RING):
                load_adj(T - ADJ_RING + r, r)
            sp.wait_ge(gathered[0], 16 * SLOTS)
            sp.dma_start(wo[:], w_o.rearrange("(k p) n -> p k n", p=P)).then_inc(late_weights_in, 16)
            sp.dma_start(b1[:], b_1).then_inc(late_weights_in, 16)
            sp.dma_start(ln1_cols[:], ln1_columns).then_inc(late_weights_in, 16)
            for r in range(4):
                sp.dma_start(ln[:, r], ln_rows[r:r + 1, :].to_broadcast([P, D])).then_inc(late_weights_in, 16)
            sp.wait_ge(gathered[1], 16 * SLOTS)
            sp.dma_start(w1[:], w_1.rearrange("(k p) n -> p k n", p=P)).then_inc(ff_weights_in, 16)
            sp.dma_start(w2[:], w_2.rearrange("(k p) n -> p k n", p=P)).then_inc(ff_weights_in, 16)

            def step(t, u, dense):
                if on(t, 0):
                    wait(sp, r1_ready, t - 1)
                    sp.dma_start(xr[:, u], x[bass.ds(t * P, P), :]).then_inc(xr_in[u], 16)
                    if dense:
                        if isinstance(t, int) and t == 0:
                            sp.wait_ge(vlist_product, 1)
                            sp.wait_ge(onehot_ready, 1)
                        wait(sp, d_mask_step, 2 * t)
                        sp.dma_start(adj_ring[:, 0], adj[bass.ds(t * P, P), :]).then_inc(dense_adj_in, 16)
                if on(t, OUT_LAG):
                    sp.wait_ge(out_ready, t - (OUT_LAG - 1))
                    sp.dma_start(out[bass.ds((t - OUT_LAG) * P, P), :], outs[:, u]).then_inc(stored[u], 16)

            both_ways(sp, lambda: steps(sp, lambda t, u: step(t, u, False)),
                      lambda: steps(sp, lambda t, u: step(t, u, True)))
            for u in range(2):
                sp.wait_ge(stored[u], 16 * T // 2)

        @block.gpsimd
        def _(pool):
            nc.gpsimd.memset(b_raw, 0.0).then_inc(bias_zeroed, 1)
            nc.gpsimd.memset(not_eye_i[:], 1).then_inc(pool_consts, 1)
            nc.gpsimd.memset(ones[:], 1.0).then_inc(pool_consts, 1)
            nc.gpsimd.memset(ones_bf[:], 1.0).then_inc(pool_consts, 1)
            nc.gpsimd.memset(eye[:], 0.0).then_inc(pool_consts, 1)
            nc.gpsimd.memset(minus_half[:], -0.5).then_inc(pool_consts, 1)
            nc.gpsimd.memset(table_end[:], float(N)).then_inc(pool_consts, 1)
            nc.gpsimd.iota(lists[:, :, LIST], [[-P, T]], base=N, channel_multiplier=-1,
                           allow_small_or_imprecise_dtypes=True).then_inc(pool_consts, 1)
            pool.wait_ge(pool_consts, 7)
            nc.gpsimd.affine_select(out=not_eye_i[:], in_=not_eye_i[:], compare_op=ALU.not_equal, fill=0.0,
                                    base=0, pattern=[[-1, P]], channel_multiplier=1).then_inc(pool_consts, 1)
            nc.gpsimd.iota(col_no[:], [[-1, N]], base=N, channel_multiplier=0,
                           allow_small_or_imprecise_dtypes=True).then_inc(pool_consts, 1)
            nc.gpsimd.affine_select(out=not_eye[:], in_=ones[:], compare_op=ALU.not_equal, fill=0.0,
                                    base=0, pattern=[[-1, P]], channel_multiplier=1).then_inc(pool_consts, 1)
            nc.gpsimd.affine_select(out=eye[:], in_=eye[:], compare_op=ALU.not_equal, fill=1.0,
                                    base=0, pattern=[[-1, P]], channel_multiplier=1).then_inc(pool_consts, 1)
            nc.gpsimd.affine_select(out=before[:], in_=ones[:], compare_op=ALU.is_gt, fill=0.0,
                                    base=0, pattern=[[1, P]], channel_multiplier=-1).then_inc(pool_consts, 1)
            pool.wait_ge(pool_consts, 12)

            def clear_diagonal(i, r):
                pool.wait_ge(adj_in[r], i * (16 // ADJ_RING) + 16)
                blk = adj_ring[:, r, bass.ds((i + r) * P, P)]
                nc.gpsimd.tensor_tensor(blk, blk, not_eye_i[:], ALU.mult).then_inc(diag_cleared, 1)

            for r in range(ADJ_RING):
                clear_diagonal(0, r)
            pool.wait_ge(bias_step, 6)
            nc.gpsimd.memset(gath[:].rearrange("p u s d -> p (u s d)"), 0.0).then_inc(gath_zeroed, 1)
            with pool.Fori(1, T // ADJ_RING) as g:
                for r in range(ADJ_RING):
                    clear_diagonal(g * ADJ_RING, r)
            for h in range(2):
                pool.wait_ge(mask_cast, T - 1 + h)
                nc.gpsimd.memset(adj_ring[:, 2 + h].bitcast(F32), 0.0).then_inc(gath_v_zeroed, 1)

            def rows_of(ix, dst, done):
                for s in range(SLOTS):
                    pool.indirect_dma_start(dst[:, s, :], None, kv_table,
                                            bass.IndirectOffsetOnAxis(ap=ix[:, s:s + 1], axis=0),
                                            bounds_check=N - 1, oob_is_err=False).then_inc(done, 16)

            def gather(t, u):
                wait_alone(pool, idx_staged, t + 1)
                if not isinstance(t, int) or t > 1:
                    wait_alone(pool, pv_ready, t - 1)
                rows_of(idx_ring[:, u], gath[:, u], gathered[u])

            def rstds(n, u, t1, t2):
                norms = slice(0 if t1 is not None else 1, 2 if t2 is not None else 1)
                if t1 is not None:
                    wait_alone(pool, mv1_ready, t1 + 1)
                if t2 is not None:
                    wait_alone(pool, mv2_ready, t2 + 1)
                nc.gpsimd.tensor_scalar(var_eps[:, u, norms], mv[:, u, norms, 1], EPS, None, ALU.add).then_inc(var_ready, 1)
                if t1 is not None:
                    nc.gpsimd.tensor_scalar(minus_mean[:, u:u + 1], mv[:, u, 0, 0:1], -1.0, None, ALU.mult).then_inc(mean1_negated, 1)
                pool.wait_ge(var_ready, n)
                nc.gpsimd.tensor_tensor(rstd[:, u, norms], var_eps[:, u, norms], minus_half[:, norms], ALU.pow).then_inc(rstd_ready, 1)

            def shift_of(t, u):
                pool.wait_ge(rstd_ready, t + 1)
                pool.wait_ge(mean1_negated, t + 1)
                nc.gpsimd.tensor_tensor(shift1[:, u:u + 1], minus_mean[:, u:u + 1], rstd[:, u, 0:1], ALU.mult).then_inc(shift1_ready, 1)

            def own(a, t):
                return a[:, t, 0:D] if isinstance(t, int) else a[:, bass.ds(t, 1), 0:D].rearrange("p a n -> p (a n)")

            def multiply_self(t):
                if not isinstance(t, int) or t > 0:
                    wait_alone(pool, scores_ready, t)
                nc.gpsimd.tensor_tensor(prod[:, SELF], own(q, t), own(kv, t), ALU.mult).then_inc(self_product, 1)

            def keep(t, u):
                row = h1keep[:, t % 4] if isinstance(t, int) else h1keep[:, bass.ds(t % 4, 1)].rearrange("p a n -> p (a n)")
                if not isinstance(t, int) or t > 3:
                    wait_alone(pool, r2_ready, t - 3)
                wait_alone(pool, normed, t + 1)
                nc.gpsimd.tensor_tensor(row, xn[:, u], ln[:, 0], ALU.mult).then_inc(h1_scaled, 1)
                wait_alone(pool, h1_scaled, t + 1)
                nc.gpsimd.tensor_tensor(row, row, ln[:, 1], ALU.add).then_inc(h1_kept, 1)

            def step(t, u, dense):
                if not dense and (not isinstance(t, int) or 1 <= t < T - 1):
                    gather(t + 1, 1 - u)
                if not dense and (not isinstance(t, int) or t < T - 1):
                    multiply_self(t + 1)
                if on(t, 2):
                    keep(t - 2, u)
                if on(t, 1) or on(t, LAG):
                    rstds(t, 1 - u, t - 1 if on(t, 1) else None, t - LAG if on(t, LAG) else None)
                if on(t, 1):
                    shift_of(t - 1, 1 - u)

            pool.wait_ge(q_stored, 2 + 1)
            multiply_self(0)
            pool.wait_ge(table_written, 16 * T)
            pool.wait_ge(gath_zeroed, 1)
            gather(0, 0)
            pool.wait_ge(gath_v_zeroed, 2)
            pool.wait_ge(vidx_ready, 1)
            rows_of(vidx[:], gath_v, v_gathered)
            gather(1, 1)

            def fast():
                for t in range(0, OUT_LAG):
                    step(t, t % 2, False)
                with pool.Fori(OUT_LAG // 2, (T - 2) // 2) as g:
                    t = g * 2
                    step(t, 0, False)
                    step(t + 1, 1, False)
                for t in range(T - 2, T + OUT_LAG):
                    step(t, t % 2, False)

            pool.wait_ge(late_weights_in, 16 * 7)
            both_ways(pool, fast, lambda: steps(pool, lambda t, u: step(t, u, True)))

        @block.tensor
        def _(pe):
            mm, tr = nc.tensor.matmul, nc.tensor.transpose

            def bias(dst, first, at):
                mm(dst, ones_bf[0:96, :], bias_parts[:, at:at + dst.shape[-1]], start=first, stop=False)

            pe.wait_ge(weights_in, 16)
            pe.wait_ge(pool_consts, 12)
            pe.wait_ge(bias_step, 6)
            with pe.Fori(0, T // ADJ_RING) as g:
                i = g * ADJ_RING
                for r in range(ADJ_RING):
                    b = r % 2
                    pe.wait_ge(xt_in[r], i * (16 // ADJ_RING) + 16)
                    pe.wait_ge(kv_stored, i + (r + 1))
                    bias(bank[b], True, 0)
                    for k in range(KD):
                        last = mm(bank[b], xt[:, r, k], wkvq[:, k, 0:2 * D], start=False, stop=k == KD - 1)
                    last.then_inc(kv_product, 1)
                    pe.wait_ge(q_stored, i + (r + 1))
                    bias(bank[2 + b][:, 0:D], True, 2 * D)
                    for k in range(KD):
                        last = mm(bank[2 + b][:, 0:D], xt[:, r, k], wkvq[:, k, 2 * D:3 * D], start=False, stop=k == KD - 1)
                    last.then_inc(q_product, 1)

            pe.wait_ge(overflow_marked, 1)
            mm(bank[7][0:T, 0:P], small[:, 0], ones[:], start=True, stop=True).then_inc(totals_summed, 1)
            mm(bank[6][:, 0:T], before[:], small[:, 0], start=True, stop=False)
            pe.wait_ge(totals_copied, 1)
            mm(bank[6][:, 0:T], vdata[0:T, 0:P], before[0:T, 0:T], start=False, stop=True).then_inc(places_summed, 1)
            pe.wait_ge(onehot16_ready, 1)
            for t in range(T):
                last = mm(bank[5][:, 0:SLOTS + 1], onehot16[:, t], lists[:, t, SLOTS:LIST + 1], start=t == 0, stop=t == T - 1)
            last.then_inc(vlist_product, 1)
            pe.wait_ge(q_stored, T + 2)
            pe.wait_ge(misses_ready, 2)
            mm(bank[3][0:1, 0:2], ones[:, 0:1], small[:, 4, 0:2], start=True, stop=True).then_inc(misses_summed, 1)
            pe.wait_ge(onehot_ready, 1)
            for t in range(T):
                last = mm(bank[4][:, 0:D], onehot[:, t], q[:, t], start=t == 0, stop=t == T - 1)
            last.then_inc(vq_product, 1)

            def sum_slots(t, u, sparse):
                wait(pe, ctx_copied, t)
                for k in range(KD):
                    for s in (*range(SLOTS - MERGED), VIRT, SELF):
                        if sparse and k == 0 and s == SELF:
                            pe.wait_ge(self_weighted, t + 1)
                        last = mm(bank[1][:, bass.ts(k, P)], pv[:, u, s, bass.ts(k, P)], eye[:],
                                  start=k == 0 and s == 0, stop=s == SELF, skip_group_check=True)
                last.then_inc(ctx_summed, 1)

            def project(t):
                pe.wait_ge(ctx_copied, t + 1)
                wait(pe, r1_ready, t)
                bias(bank[2][:, 0:D], True, 3 * D)
                for k in range(KD):
                    last = mm(bank[2][:, 0:D], ctx_t[:, k], wo[:, k], start=False, stop=k == KD - 1)
                last.then_inc(wo_done, 1)

            def first_layer(t, g, blocks=range(2)):
                if blocks[0] == 0:
                    wait(pe, relu_done, 2 * t + g - 1)
                for j in blocks:
                    for k in range(KD):
                        f = 2 * g + j
                        last = mm(bank[4 + g % 2][:, bass.ts(j, 2 * P)], w1[:, k, bass.ts(f, P)],
                                  h1_t[:, k].rearrange("p a b -> p (a b)"),
                                  start=k == 0 and j == 0, stop=k == KD - 1, skip_group_check=True)
                if blocks[-1] == 1:
                    last.then_inc(ff1_ready, 1)

            def second_layer(v, blocks):
                for f in blocks:
                    last = mm(bank[6 + v][:, 0:D], hid[:, f, v], w2[:, f], start=False, stop=f == FB - 1)
                    if f == FB - 1:
                        last.then_inc(ff2_done, 1)

            def turn_norm(t, u):
                pe.wait_ge(normed, t + 1)
                wait(pe, h1_copied, t)
                for k in range(KD):
                    last = tr(bank[3][:, bass.ts(k, P)], xn[:, u, bass.ts(k, P)], eye[:])
                last.then_inc(h1_turned, 1)

            def post(t, u, first=None):
                w = 1 - u
                if on(t, 1):
                    pe.wait_ge(pv_ready, t)
                    if first and on(t, 0):
                        first(t, u)
                    sum_slots(t - 1, w, first is not None)
                if first and isinstance(t, int) and t in (2, 3):
                    turn_norm(t - 2, u)
                if u == 1 and on(t, 3):
                    if isinstance(t, int) and t == 3:
                        pe.wait_ge(ff_weights_in, 16 * 2)
                    pe.wait_ge(h1_copied, t - 1)
                    first_layer(t - 3, 0, range(1))
                    if on(t, 1):
                        project(t - 1)
                    first_layer(t - 3, 0, range(1, 2))
                    for g in range(1, FB // 2):
                        first_layer(t - 3, g)
                elif u == 0 and on(t, 4):
                    pe.wait_ge(relu_done, 2 * (t - 4) + FB // 2)
                    wait(pe, r2_ready, t - 5)
                    bias(bank[6][:, 0:D], True, 4 * D)
                    second_layer(0, range(2))
                    if on(t, 1):
                        project(t - 1)
                    second_layer(0, range(2, FB))
                    wait(pe, r2_ready, t - 4)
                    bias(bank[7][:, 0:D], True, 4 * D)
                    second_layer(1, range(FB))
                elif on(t, 1):
                    project(t - 1)
                if on(t, 1) and not (first and isinstance(t, int) and t < 3):
                    turn_norm(t - 1, w)

            def fetch_virtual(t, u):
                pe.wait_ge(turned_ready, t + 1)
                wait(pe, pv_ready, t)
                mm(bank[0][:, 0:VCOLS], turned[:, u], vdata[:], start=True, stop=True).then_inc(merged, 1)

            def fast():
                pe.wait_ge(v_done, 1)
                fetch_virtual(0, 0)

                pe.wait_ge(late_weights_in, 16 * 7)
                steps(pe, lambda t, u: post(t, u, fetch_virtual))

            def dense():
                pe.wait_ge(late_weights_in, 16 * 7)

                def heads(t):
                    if not isinstance(t, int) or t > 1:
                        wait_alone(pe, ctx_copied, t - 1)
                    with pe.Fori(0, H) as h:
                        n = t * H + h
                        k0, m0 = n * 10, n * 14
                        pe.wait_ge(d_staged, k0 + 1)
                        tr(bank[1][0:DK, 0:P], d_q, eye[:]).then_inc(d_product, 1)
                        for c in range(4):
                            pe.wait_ge(d_staged, k0 + 2 + c)
                            for j in range(4):
                                last = tr(bank[1][0:DK, bass.ts(j, P)], d_k[:, 4 * c + j], eye[:])
                            last.then_inc(d_product, 1)
                            pe.wait_ge(d_staged, k0 + 3 + c)
                            mm(bank[0], d_qt, d_t[0:DK], start=True, stop=True).then_inc(d_product, 1)
                        pe.wait_ge(d_exp, n + 1)
                        for c in range(4):
                            if c:
                                pe.wait_ge(d_staged, k0 + 6 + c)
                            for j in range(4):
                                last = tr(bank[1][:, bass.ts(j, P)], d_p[:, bass.ts(4 * c + j, P)], eye[:])
                            last.then_inc(d_product, 1)
                            pe.wait_ge(d_staged, k0 + 7 + c)
                            for j in range(4):
                                m = 4 * c + j
                                last = mm(bank[0][:, 0:DK], d_t[:, bass.ts(j, P)],
                                          kv[:, m, bass.ds(h * DK + D, DK)], start=m == 0, stop=m == T - 1)
                        last.then_inc(d_product, 1)

                def step(t, u):
                    if on(t, 0):
                        heads(t)
                    post(t, u)
                steps(pe, step)

            both_ways(pe, fast, dense)

        @block.scalar
        def _(act):
            af = nc.scalar.activation
            def cast(t, r):
                act.wait_ge(diag_cleared, t + 1)
                act.wait_ge(cands_ready, t + 1)
                af(coded[:, r], adj_ring[:, r], ACT.Sign, accum_out=count[:, bass.ds(t, 1)]).then_inc(mask_cast, 1)

            def projected(i):
                for u in range(2):
                    kv_rows = kv[:, bass.ds(i + u, 1)].rearrange("p a n -> p (a n)")
                    act.wait_ge(kv_product, i + (u + 1))
                    af(kv_rows, bank[u], ACT.Copy).then_inc(kv_stored, 1)
                    act.wait_ge(q_product, i + (u + 1))
                    af(q[:, bass.ds(i + u, 1)].rearrange("p a n -> p (a n)"), bank[2 + u][:, 0:D], ACT.Copy).then_inc(q_stored, 1)
                    act.wait_ge(kv_stored, i + (u + 3))
                    act.dma_start(kv_table[bass.ds((i + u) * P, P), :], kv_rows).then_inc(table_written, 16)

            cast(0, 0)
            cast(1, 1)
            with act.Fori(0, T // ADJ_RING - 1) as g:
                i = g * ADJ_RING
                cast(i + 2, 2)
                cast(i + 3, 3)
                projected(i)
                cast(i + 4, 0)
                cast(i + 5, 1)
                projected(i + 2)
            cast(T - 2, 2)
            projected(T - 4)
            cast(T - 1, 3)
            projected(T - 2)

            def index(dst, codes, done):
                af(dst, codes, ACT.Identity, bias=table_end[:, 0:1], scale=-1.0).then_inc(done, 1)

            def stage_idx(t, u):
                wait(act, gathered[u], (t - u) * (SLOTS * 8))
                src = lists[:, t, 0:SLOTS] if isinstance(t, int) else lists[:, bass.ds(t, 1), 0:SLOTS].rearrange("p a s -> p (a s)")
                index(idx_ring[:, u], src, idx_staged)

            act.wait_ge(lists_done, 1)
            stage_idx(0, 0)
            stage_idx(1, 1)
            act.wait_ge(vlist_product, 1)
            index(vidx[:], bank[5][:, 0:SLOTS], vidx_ready)
            af(onehot.rearrange("p t n -> p (t n)"), onehot16.rearrange("p t n -> p (t n)"), ACT.Copy).then_inc(onehot_ready, 1)

            def ctx_copy(t, u):
                act.wait_ge(ctx_summed, t + 1)
                wait(act, wo_done, t)
                af(ctx_t[:].rearrange("p a b -> p (a b)"), bank[1][:, 0:D], ACT.Copy).then_inc(ctx_copied, 1)

            def relu(t, g):
                act.wait_ge(ff1_ready, 2 * (t - 3) + g + 1)
                if g == 0:
                    wait(act, ff2_done, t - 3)
                for j in range(2):
                    f = 2 * g + j
                    last = af(hid[:, f].rearrange("p a b -> p (a b)"), bank[4 + g % 2][:, bass.ts(j, 2 * P)],
                              ACT.Relu, bias=b1[:, f:f + 1])
                last.then_inc(relu_done, 1)

            def normalize(t, u):
                act.wait_ge(shift1_ready, t + 1)
                wait(act, h1_turned, t - 1)
                wait(act, h1_scaled, t - 1)
                af(xn[:, u], r1[:, u], ACT.Identity, bias=shift1[:, u:u + 1], scale=rstd[:, u, 0:1]).then_inc(normed, 1)

            def h1_copy(t, u):
                act.wait_ge(h1_turned, t + 1)
                wait(act, ff1_ready, 2 * (t - u))
                for k in range(KD):
                    last = af(h1_t[:, k, u], bank[3][:, bass.ts(k, P)], ACT.Identity,
                              bias=ln1_cols[:, KD + k:KD + k + 1], scale=ln1_cols[:, k:k + 1])
                last.then_inc(h1_copied, 1)

            def weigh_self(t, u):
                act.wait_ge(weights_ready, t + 1)
                wait(act, ctx_summed, t - 1)
                for h in range(H):
                    row = slice(D + h * DK, D + (h + 1) * DK)
                    own = kv[:, t, row] if isinstance(t, int) else kv[:, bass.ds(t, 1), row].rearrange("p a n -> p (a n)")
                    last = af(pv[:, u, SELF, bass.ts(h, DK)], own, ACT.Copy, scale=wts[:, SELF, h:h + 1])
                last.then_inc(self_weighted, 1)

            def post(t, u, sparse):
                hidden = u == 1 and on(t, 3)
                if hidden:
                    for g in range(FB // 2 - 2):
                        relu(t, g)
                if sparse and on(t, 0):
                    weigh_self(t, u)
                if hidden:
                    relu(t, FB // 2 - 2)
                if on(t, 1):
                    normalize(t - 1, 1 - u)
                if hidden:
                    relu(t, FB // 2 - 1)
                if on(t, 1):
                    h1_copy(t - 1, 1 - u)

            def fast():
                act.wait_ge(v_shifted, 1)
                af(ex[:, 0:SLOTS].rearrange("p s h -> p (s h)"), sc[:, 1, 0:SLOTS].rearrange("p s h -> p (s h)"),
                   ACT.Exp, scale=SCALE).then_inc(v_exp, 1)

                def step(t, u):
                    if on(t, 1):
                        ctx_copy(t - 1, 1 - u)
                    if on(t, 0):
                        act.wait_ge(shifted, t + 1)
                        af(ex[:].rearrange("p s h -> p (s h)"), sc[:, u].rearrange("p s h -> p (s h)"),
                           ACT.Exp, scale=SCALE).then_inc(exp_done, 1)
                    if not isinstance(t, int) or t < T - 2:
                        stage_idx(t + 2, u)
                    post(t, u, True)

                act.wait_ge(late_weights_in, 16 * 7)
                for t in range(0, OUT_LAG):
                    step(t, t % 2)
                with act.Fori(OUT_LAG // 2, (T - 2) // 2) as g:
                    t = g * 2
                    step(t, 0)
                    step(t + 1, 1)
                for t in range(T - 2, T + OUT_LAG):
                    step(t, t % 2)

            def dense():
                act.wait_ge(late_weights_in, 16 * 7)

                def step(t, u):
                    if on(t, 0):
                        with act.Fori(0, H) as h:
                            act.wait_ge(d_max, t * H + h + 1)
                            af(d_p, d_sc, ACT.Exp, bias=mx[:, 0:1], scale=SCALE, accum_out=lsum[:, 0:1]).then_inc(d_exp, 1)
                    if on(t, 1):
                        ctx_copy(t - 1, 1 - u)
                    post(t, u, False)
                steps(act, step)

            both_ways(act, fast, dense)

        @block.vector
        def _(dve):
            v = nc.vector
            v.memset(small[:, 7, 1:2], 0.0).then_inc(kv_stored, 2)
            v.memset(small[:, 7, 2:3], 0.0).then_inc(q_stored, 2)
            v.memset(small[:, 7, 3:4], 0.0).then_inc(cands_ready, CODE_RING)
            dve.wait_ge(biases_in, 48)
            v.tensor_copy(b_hi, b_raw).then_inc(bias_step, 1)
            dve.wait_ge(bias_step, 1)
            v.tensor_tensor(b_rest, b_raw, b_hi, ALU.subtract).then_inc(bias_step, 1)
            dve.wait_ge(bias_step, 2)
            v.tensor_copy(b_mid, b_rest).then_inc(bias_step, 1)
            dve.wait_ge(bias_step, 3)
            v.tensor_copy(bias_parts[0:32, :], b_hi[0:32]).then_inc(bias_step, 1)
            v.tensor_copy(bias_parts[32:64, :], b_mid[32:64]).then_inc(bias_step, 1)
            v.tensor_tensor(bias_parts[64:96, :], b_rest[64:96], b_mid[64:96], ALU.subtract).then_inc(bias_step, 1)

            def first_8(i, pair, u):
                wait_alone(dve, cands_ready, i + (u + 1 + CODE_RING))
                v.max(top[:, u, 0:8], cand[:, pair + u]).then_inc(tops_ready, 1)

            def without_them(i, pair, u):
                wait_alone(dve, tops_ready, i + (u + 1))
                v.match_replace(cand_rest[:, u], top[:, u, 0:8], cand[:, pair + u], 0.0).then_inc(rest_ready, 1)

            def second_8(i, u):
                wait_alone(dve, rest_ready, i + (u + 1))
                v.max(top[:, u, 8:16], cand_rest[:, u]).then_inc(listed, 1)

            def keep_lists(i):
                dve.wait_ge(listed, i + 2)
                v.tensor_copy(lists[:, bass.ds(i, 2), 0:LIST], top[:]).then_inc(lists_done, 1)

            def code(i, pair, u):
                dve.wait_ge(mask_cast, i + (u + 1))
                v.tensor_tensor(coded[:, pair + u], coded[:, pair + u], col_no[:], ALU.mult).then_inc(coded_ready, 1)

            def candidates(pair, u, c):
                return v.max(cand[:, pair + u, bass.ts(c, 8)], coded[:, pair + u, bass.ts(c, QUARTER)])

            def scan(i, pair, others):
                code(i, pair, 0)
                code(i, pair, 1)
                wait_alone(dve, coded_ready, i + 1)
                for c in range(4):
                    last = candidates(pair, 0, c)
                    if c == 3:
                        last.then_inc(cands_ready, 1)
                    if others and c < 2:
                        first_8(i - 2, 2 - pair, c)
                    elif others:
                        without_them(i - 2, 2 - pair, c - 2)
                wait_alone(dve, coded_ready, i + 2)
                for c in range(4):
                    last = candidates(pair, 1, c)
                    if c == 3:
                        last.then_inc(cands_ready, 1)
                    if others and c < 2:
                        second_8(i - 2, c)
                    elif others and c == 2:
                        keep_lists(i - 2)

            dve.wait_ge(pool_consts, 12)
            scan(0, 0, False)
            scan(2, 2, True)
            with dve.Fori(1, T // CODE_RING) as g:
                scan(g * CODE_RING, 0, True)
                scan(g * CODE_RING + 2, 2, True)
            dve.wait_ge(lists_done, T // 2 - 1)
            for u in range(2):
                first_8(T - 2, 2, u)
            for u in range(2):
                without_them(T - 2, 2, u)
            for u in range(2):
                second_8(T - 2, u)
            keep_lists(T - 2)

            dve.wait_ge(lists_done, T // 2)
            v.tensor_scalar(small[:, 0], lists[:, :, SLOTS], 0.0, None, ALU.is_gt).then_inc(overflow_marked, 1)
            v.tensor_scalar(small[:, 6], lists[:, :, SLOTS], 0.0, -1.0, ALU.is_gt, ALU.mult).then_inc(overflow_marked, 1)
            present = prod[:, 0, 0:T * LIST].rearrange("p (t s) -> p t s", s=LIST)
            v.tensor_scalar(present, lists[:, :, 0:LIST], 0.0, None, ALU.is_gt).then_inc(listed_count, 1)
            dve.wait_ge(totals_summed, 1)
            v.tensor_copy(vdata[0:T, 0:P], bank[7][0:T, 0:P]).then_inc(totals_copied, 1)
            dve.wait_ge(listed_count, 1)
            v.tensor_reduce(small[:, 1], present, AX.X, ALU.add).then_inc(listed_count, 1)
            v.tensor_reduce(small[:, 4, 1:2], small[:, 0], AX.X, ALU.add).then_inc(misses_ready, 1)
            dve.wait_ge(places_summed, 1)
            dve.wait_ge(overflow_marked, 2)
            v.scalar_tensor_tensor(out=small[:, 3], in0=bank[6][:, 0:T], scalar=float(N), in1=small[:, 6],
                                   op0=ALU.subtract, op1=ALU.mult).then_inc(place_ready, 1)
            dve.wait_ge(place_ready, 1)
            v.tensor_tensor(onehot16, col_no[:, 0:P].unsqueeze(1).to_broadcast([P, T, P]),
                            small[:, 3].unsqueeze(2).to_broadcast([P, T, P]), ALU.is_equal).then_inc(onehot16_ready, 1)
            dve.wait_ge(listed_count, 2)
            v.tensor_tensor(small[:, 2], count[:], small[:, 1], ALU.not_equal).then_inc(listed_count, 1)
            dve.wait_ge(listed_count, 3)
            v.tensor_reduce(small[:, 4, 0:1], small[:, 2], AX.X, ALU.add).then_inc(misses_ready, 1)
            v.tensor_scalar(mask[:], lists[:, :, 0:SLOTS], 0.0, MASKED, ALU.is_equal, ALU.mult).then_inc(v_step, 1)
            dve.wait_ge(misses_summed, 1)
            v.tensor_scalar(small[0:1, 5, 0:1], bank[3][0:1, 0:1], 0.0, None, ALU.is_gt).then_inc(v_step, 1)
            v.tensor_scalar(small[0:1, 5, 1:2], bank[3][0:1, 1:2], float(P), None, ALU.is_gt).then_inc(v_step, 1)
            dve.wait_ge(v_step, 3)
            v.tensor_tensor(flag_i[:], small[0:1, 5, 0:1], small[0:1, 5, 1:2], ALU.max).then_inc(flag_ready, 1)

            def ln1_add(t, u):
                dve.wait_ge(wo_done, t + 1)
                dve.wait_ge(xr_in[u], (t - u) * 8 + 16)
                v.tensor_tensor(r1[:, u], bank[2][:, 0:D], xr[:, u], ALU.add).then_inc(r1_ready, 1)

            def ln1_stats(t, u):
                dve.wait_ge(r1_ready, t + 1)
                v.bn_stats(stats[:, 0], r1[:, u]).then_inc(stats1, 1)

            def ln1_mean(t, u):
                wait_alone(dve, stats1, t + 1)
                v.bn_aggr(mv[:, u, 0], stats[:, 0]).then_inc(mv1_ready, 1)

            def ln2_add(t, u):
                row = h1keep[:, t % 4] if isinstance(t, int) else h1keep[:, bass.ds(t % 4, 1)].rearrange("p a n -> p (a n)")
                dve.wait_ge(ff2_done, t + 1)
                dve.wait_ge(h1_kept, t + 1)
                v.tensor_tensor(r2[:, u], bank[6 + u][:, 0:D], row, ALU.add).then_inc(r2_ready, 1)

            def ln2_stats(t, u):
                dve.wait_ge(r2_ready, t + 1)
                v.bn_stats(stats[:, 1], r2[:, u]).then_inc(stats2, 1)

            def ln2_mean(t, u):
                wait_alone(dve, stats2, t + 1)
                v.bn_aggr(mv[:, u, 1], stats[:, 1]).then_inc(mv2_ready, 1)

            def ln2_half(t, u):
                dve.wait_ge(rstd_ready, t + LAG)
                wait(dve, out_ready, t)
                v.scalar_tensor_tensor(out=lntmp[:], in0=r2[:, u], scalar=mv[:, u, 1, 0:1], in1=ln[:, 2],
                                       op0=ALU.subtract, op1=ALU.mult).then_inc(half2, 1)

            def ln2_out(t, u):
                wait(dve, stored[u], (t - u) * 8)
                dve.wait_ge(half2, t + 1)
                v.scalar_tensor_tensor(out=outs[:, u], in0=lntmp[:], scalar=rstd[:, u, 1:2], in1=ln[:, 3],
                                       op0=ALU.mult, op1=ALU.add).then_inc(out_ready, 1)

            def turn(t, u):
                wait(dve, merged, t - 1)
                src = col_no[:, bass.ts(t, P)] if isinstance(t, int) else col_no[:, bass.ds(t * P, P)]
                v.tensor_scalar(turned[:, u], src, vlist[:, SLOTS:SLOTS + 1], None, ALU.is_equal).then_inc(turned_ready, 1)

            def tile_of(a, t, *rest):
                if isinstance(t, int):
                    return a[(slice(None), t) + rest]
                return a[(slice(None), bass.ds(t, 1)) + rest].rearrange("p a n -> p (a n)")

            def products(t, u):
                dve.wait_ge(gathered[u], (t - u) * (SLOTS * 8) + 16 * SLOTS)
                qt = tile_of(q, t)
                v.tensor_tensor(prod[:, 0:SLOTS], gath[:, u, :, 0:D], qt.unsqueeze(1).to_broadcast([P, SLOTS, D]), ALU.mult).then_inc(prods_ready, 1)

            def scores(t, u):
                dve.wait_ge(prods_ready, t + 1)
                dve.wait_ge(self_product, t + 1)
                v.tensor_reduce(sc[:, u, 0:SLOTS + 1].rearrange("p s h -> p (s h)"),
                                prod[:].rearrange("p s (h d) -> p (s h) d", d=DK), AX.X, ALU.add).then_inc(scores_ready, 1)

            def virtual_absent(t, u):
                dve.wait_ge(merged, t + 1)
                v.tensor_scalar(absent[:], bank[0][:, VCOLS - 1:VCOLS], -MASKED, MASKED, ALU.mult, ALU.add).then_inc(absent_ready, 1)

            def virtual_max(t, u):
                dve.wait_ge(absent_ready, t + 1)
                v.tensor_scalar(sc[:, u, VIRT], bank[0][:, D:D + H], absent[:, 0:1], None, ALU.add).then_inc(masked_scores, 1)

            def mask_scores(t, u):
                dve.wait_ge(scores_ready, t + 1)
                v.tensor_tensor(sc[:, u, 0:SLOTS], sc[:, u, 0:SLOTS],
                                tile_of(mask, t).unsqueeze(2).to_broadcast([P, SLOTS, H]), ALU.add).then_inc(masked_scores, 1)

            def maximum(t, u):
                dve.wait_ge(masked_scores, t * 2 + 2)
                v.tensor_reduce(mx[:], sc[:, u].rearrange("p s h -> p h s"), AX.X, ALU.max).then_inc(max_ready, 1)

            def shift(t, u):
                dve.wait_ge(max_ready, t + 1)
                v.tensor_tensor(sc[:, u], sc[:, u], mx[:].unsqueeze(1).to_broadcast([P, ALLS, H]), ALU.subtract).then_inc(shifted, 1)

            def virtual_sum(t, u):
                dve.wait_ge(exp_done, t + 1)
                v.tensor_tensor(ex[:, VIRT], ex[:, VIRT], bank[0][:, D + H:D + 2 * H], ALU.mult).then_inc(virtual_scaled, 1)

            def sums(t, u):
                dve.wait_ge(virtual_scaled, t + 1)
                v.tensor_reduce(lsum[:], ex[:].rearrange("p s h -> p h s"), AX.X, ALU.add).then_inc(sums_ready, 1)

            def inverse(t, u):
                dve.wait_ge(sums_ready, t + 1)
                v.reciprocal(rinv[:], lsum[:]).then_inc(inverse_ready, 1)

            def weights(t, u):
                dve.wait_ge(inverse_ready, t + 1)
                wait(dve, self_weighted, t)
                v.tensor_tensor(wts[:], ex[:], rinv[:].unsqueeze(1).to_broadcast([P, ALLS, H]), ALU.mult).then_inc(weights_ready, 1)

            def weigh(t, u):
                wait(dve, ctx_summed, t - 1)
                dve.wait_ge(weights_ready, t + 1)
                v.tensor_tensor(pv[:, u, VIRT].rearrange("p (h d) -> p h d", d=DK), bank[0][:, 0:D].rearrange("p (h d) -> p h d", d=DK),
                                wts[:, VIRT].unsqueeze(2).to_broadcast([P, H, DK]), ALU.mult)
                v.tensor_tensor(pv[:, u, 0:SLOTS].rearrange("p s (h d) -> p s h d", d=DK),
                                gath[:, u, :, D:2 * D].rearrange("p s (h d) -> p s h d", d=DK),
                                wts[:, 0:SLOTS].unsqueeze(3).to_broadcast([P, SLOTS, H, DK]), ALU.mult).then_inc(weighted, 1)

            def merge_slots(t, u):
                dve.wait_ge(weighted, t + 1)
                v.tensor_tensor(pv[:, u, 0:MERGED], pv[:, u, 0:MERGED], pv[:, u, SLOTS - MERGED:SLOTS], ALU.add).then_inc(pv_ready, 1)

            def step(t, u):
                w = 1 - u
                now, ln1, ln2, ln2_end = on(t, 0), on(t, 1), on(t, LAG), on(t, OUT_LAG)
                first = isinstance(t, int) and t == 0
                early = isinstance(t, int) and t < WARM
                if now and not (isinstance(t, int) and t < 2):
                    products(t, u)
                if ln2_end:
                    ln2_half(t - OUT_LAG, u)
                if now and not first:
                    scores(t, u)
                if now:
                    virtual_absent(t, u)
                if ln2_end:
                    ln2_out(t - OUT_LAG, u)
                if now:
                    mask_scores(t, u)
                    virtual_max(t, u)
                if ln2:
                    ln2_add(t - LAG, w)
                if now:
                    maximum(t, u)
                if ln2:
                    ln2_stats(t - LAG, w)
                if now:
                    shift(t, u)
                if not isinstance(t, int) or t < T - 1:
                    turn(t + 1, w)
                if ln1 and not early:
                    ln1_add(t - 1, w)
                if now:
                    virtual_sum(t, u)
                if ln1 and not early:
                    ln1_stats(t - 1, w)
                if now:
                    sums(t, u)
                if ln2:
                    ln2_mean(t - LAG, w)
                if now:
                    inverse(t, u)
                if ln1 and not early:
                    ln1_mean(t - 1, w)
                if now:
                    weights(t, u)
                    weigh(t, u)
                    merge_slots(t, u)
                if ln1 and early:
                    ln1_add(t - 1, w)
                    ln1_stats(t - 1, w)
                    ln1_mean(t - 1, w)

            def fast():
                dve.wait_ge(vidx_ready, 1)
                v.tensor_copy(vlist[:], bank[5][:, 0:SLOTS + 1]).then_inc(v_step, 1)
                dve.wait_ge(v_step, 4)
                v.tensor_scalar(vmask[:], vlist[:, 0:SLOTS], 0.0, MASKED, ALU.is_equal, ALU.mult).then_inc(v_step, 1)
                turn(0, 0)
                products(0, 0)
                scores(0, 0)
                dve.wait_ge(vq_product, 1)
                v.tensor_copy(vq[:], bank[4][:, 0:D]).then_inc(v_step, 1)
                vsc = sc[:, 1, 0:SLOTS]
                dve.wait_ge(v_gathered, 16 * SLOTS)
                dve.wait_ge(v_step, 6)
                dve.wait_ge(scores_ready, 1)
                v.tensor_tensor(prod[:, 0:SLOTS], gath_v[:, :, 0:D], vq[:].unsqueeze(1).to_broadcast([P, SLOTS, D]), ALU.mult).then_inc(v_step, 1)
                dve.wait_ge(v_step, 7)
                v.tensor_reduce(vsc.rearrange("p s h -> p (s h)"),
                                prod[:, 0:SLOTS].rearrange("p s (h d) -> p (s h) d", d=DK), AX.X, ALU.add).then_inc(v_step, 1)
                dve.wait_ge(v_step, 8)
                v.tensor_tensor(vsc, vsc, vmask[:].unsqueeze(2).to_broadcast([P, SLOTS, H]), ALU.add).then_inc(v_step, 1)
                dve.wait_ge(v_step, 9)
                v.tensor_reduce(vdata[:, D:D + H], vsc.rearrange("p s h -> p h s"), AX.X, ALU.max).then_inc(v_step, 1)
                dve.wait_ge(v_step, 10)
                v.tensor_tensor(vsc, vsc, vdata[:, D:D + H].unsqueeze(1).to_broadcast([P, SLOTS, H]), ALU.subtract).then_inc(v_shifted, 1)
                v.memset(vdata[:, VCOLS - 1:VCOLS], 1.0).then_inc(v_step, 1)
                dve.wait_ge(v_exp, 1)
                v.tensor_reduce(vdata[:, D + H:D + 2 * H], ex[:, 0:SLOTS].rearrange("p s h -> p h s"), AX.X, ALU.add).then_inc(v_step, 1)
                dve.wait_ge(v_step, 12)
                v.reciprocal(rinv[:], vdata[:, D + H:D + 2 * H]).then_inc(v_step, 1)
                dve.wait_ge(v_step, 13)
                v.tensor_tensor(wts[:, 0:SLOTS], ex[:, 0:SLOTS], rinv[:].unsqueeze(1).to_broadcast([P, SLOTS, H]), ALU.mult).then_inc(v_step, 1)
                dve.wait_ge(v_step, 14)
                v.tensor_tensor(pv[:, 0, 0:SLOTS].rearrange("p s (h d) -> p s h d", d=DK),
                                gath_v[:, :, D:2 * D].rearrange("p s (h d) -> p s h d", d=DK),
                                wts[:, 0:SLOTS].unsqueeze(3).to_broadcast([P, SLOTS, H, DK]), ALU.mult).then_inc(v_step, 1)
                dve.wait_ge(v_step, 15)
                v.tensor_reduce(vdata[:, 0:D], pv[:, 0, 0:SLOTS].rearrange("p s d -> p d s"), AX.X, ALU.add).then_inc(v_done, 1)

                products(1, 1)
                for t in range(0, OUT_LAG):
                    if t == 2:
                        dve.wait_ge(late_weights_in, 16 * 7)
                    step(t, t % 2)
                with dve.Fori(OUT_LAG // 2, (T - 2) // 2) as g:
                    t = g * 2
                    step(t, 0)
                    step(t + 1, 1)
                for t in range(T - 2, T + OUT_LAG):
                    step(t, t % 2)

            def dense():
                dve.wait_ge(v_gathered, 16 * SLOTS)
                dve.wait_ge(vq_product, 1)
                dve.wait_ge(late_weights_in, 16 * 7)
                v.memset(pv[:].rearrange("p u s d -> p (u s d)"), 0.0).then_inc(v_step, 1)
                dve.wait_ge(v_step, 4)

                def attend(t, u):
                    dve.wait_ge(dense_adj_in, t * 16 + 16)
                    v.tensor_scalar(d_mask, adj_ring[:, 0], 0.0, MASKED, ALU.is_equal, ALU.mult).then_inc(d_mask_step, 1)
                    dve.wait_ge(d_mask_step, t * 2 + 1)
                    blk = d_mask[:, bass.ds(t * P, P)]
                    v.tensor_tensor(blk, blk, not_eye[:], ALU.mult).then_inc(d_mask_step, 1)
                    wait_alone(dve, d_mask_step, t * 2 + 2)
                    if not isinstance(t, int) or t > 1:
                        wait_alone(dve, ctx_summed, t - 1)
                    with dve.Fori(0, H) as h:
                        n = t * H + h
                        k0, m0 = n * 10, n * 14
                        v.tensor_copy(d_k, kv[:, :, bass.ds(h * DK, DK)])
                        qh = q[:, bass.ds(t, 1), bass.ds(h * DK, DK)].rearrange("p a n -> p (a n)")
                        v.tensor_copy(d_q, qh).then_inc(d_staged, 1)
                        dve.wait_ge(d_product, m0 + 1)
                        v.tensor_copy(d_qt, bank[1][0:DK, 0:P]).then_inc(d_staged, 1)
                        for c in range(4):
                            dve.wait_ge(d_product, m0 + 2 + 2 * c)
                            v.tensor_copy(d_t[0:DK], bank[1][0:DK]).then_inc(d_staged, 1)
                            dve.wait_ge(d_product, m0 + 3 + 2 * c)
                            last = v.tensor_tensor(d_sc[:, bass.ts(c, 512)], bank[0], d_mask[:, bass.ts(c, 512)], ALU.add)
                        last.then_inc(d_inv, 1)
                        dve.wait_ge(d_inv, n * 3 + 1)
                        v.tensor_reduce(rinv[:, 0:1], d_sc, AX.X, ALU.max).then_inc(d_inv, 1)
                        dve.wait_ge(d_inv, n * 3 + 2)
                        v.tensor_scalar(mx[:, 0:1], rinv[:, 0:1], -SCALE, None, ALU.mult).then_inc(d_max, 1)
                        dve.wait_ge(d_exp, n + 1)
                        v.reciprocal(rinv[:, 1:2], lsum[:, 0:1]).then_inc(d_inv, 1)
                        for c in range(4):
                            dve.wait_ge(d_product, m0 + 10 + c)
                            v.tensor_copy(d_t, bank[1]).then_inc(d_staged, 1)
                        dve.wait_ge(d_product, m0 + 14)
                        dve.wait_ge(d_inv, n * 3 + 3)
                        v.tensor_scalar(pv[:, u, 0, bass.ds(h * DK, DK)], bank[0][:, 0:DK], rinv[:, 1:2], None, ALU.mult).then_inc(d_done, 1)
                    dve.wait_ge(d_done, t * H + H)
                    v.memset(absent[:], 0.0).then_inc(pv_ready, 1)

                def step(t, u):
                    if on(t, 0):
                        attend(t, u)
                    if on(t, 1):
                        ln1_add(t - 1, 1 - u)
                        ln1_stats(t - 1, 1 - u)
                        ln1_mean(t - 1, 1 - u)
                    if on(t, LAG):
                        ln2_add(t - LAG, 1 - u)
                        ln2_stats(t - LAG, 1 - u)
                        ln2_mean(t - LAG, 1 - u)
                    if on(t, OUT_LAG):
                        ln2_half(t - OUT_LAG, u)
                        ln2_out(t - OUT_LAG, u)
                steps(dve, step)

            dve.wait_ge(q_stored, T + 2)
            dve.wait_ge(kv_stored, T + 2)
            both_ways(dve, fast, dense)


def kernel(**inputs):
    import numpy as np
    import concourse.bacc as bacc
    from concourse import mybir as mb
    from concourse.bass_utils import run_bass_kernel_spmd

    a = {k.removeprefix("L0_gnn_"): np.asarray(v) for k, v in inputs.items()}
    x = a["x"]
    laid = {
        "x": x,
        "x_t": x.reshape(16, 128, 2, 128).transpose(0, 3, 2, 1).reshape(16, 128, 256),
        "adj": a["adj"],
        "w_kvq": np.concatenate([a["Wk"].T, a["Wv"].T, a["Wq"].T], axis=1),
        "bias_row": np.concatenate([a["bk"], a["bv"], a["bq"], a["bo"], a["b2"]])[None, :],
        "w_o": a["Wo"].T,
        "w_1": a["W1"].T,
        "b_1": a["b1"].reshape(8, 128).T,
        "w_2": a["W2"].T,
        "ln_rows": np.stack([a["ln1_g"], a["ln1_b"], a["ln2_g"], a["ln2_b"]]),
        "ln1_columns": np.concatenate([a["ln1_g"].reshape(2, 128), a["ln1_b"].reshape(2, 128)]).T,
    }
    nc = bacc.Bacc("TRN2", target_bir_lowering=False, num_devices=1)
    arrays, args = {}, []
    for name, v in laid.items():
        v = np.ascontiguousarray(v)
        arrays[f"in_{name}_dram"] = v
        args.append(nc.dram_tensor(f"in_{name}_dram", v.shape, mb.dt.from_np(v.dtype), kind="ExternalInput").ap())
    out = nc.dram_tensor("out_0_dram", (2048, 256), mb.dt.float32, kind="ExternalOutput").ap()
    build(nc, *args, out)
    r = run_bass_kernel_spmd(nc, [arrays], core_ids=[0])
    return r.results[0]["out_0_dram"]
```
